# Optimizing a Trainium2 kernel written in Bass

```python
import numpy as np
import jax
import jax.numpy as jnp

def _softmax(x, axis=-1):
    return jax.nn.softmax(x, axis=axis)

def _gelu(x):
    return jax.nn.gelu(x, approximate=True)

def _silu(x):
    return jax.nn.silu(x)

def _sigmoid(x):
    return jax.nn.sigmoid(x)

def _layernorm(x, axis=-1, eps=1e-05):
    m = jnp.mean(x, axis=axis, keepdims=True)
    v = jnp.var(x, axis=axis, keepdims=True)
    return (x - m) / jnp.sqrt(v + eps)

def _scatter_add(tgt, idx, src, axis=0):
    return tgt.at[idx].add(src)

def _segment_sum(src, seg, n):
    return jax.ops.segment_sum(src, seg, n)
kernel_name = 'mk_decoder_postln_d1_seqx_r8_b02db5'

def setup_inputs(seed: int=0):
    np.random.seed(seed)
    _w = jnp.asarray

    def _rec_inputs():
        import jax
        import jax.numpy as jnp
        _rk = jax.random.key(seed)
        x = -0.000125 + 0.9999 * jax.random.normal(jax.random.fold_in(_rk, 1), (64, 128, 128), jnp.float32)
        _lenS = 128 - jax.random.randint(jax.random.fold_in(_rk, 7), (64,), 0, max(1, 128 // 4) + 1, jnp.int32)
        _lenS2 = 120 - jax.random.randint(jax.random.fold_in(_rk, 8), (64,), 0, max(1, 120 // 4) + 1, jnp.int32)
        _ctx_1024P = jax.random.normal(jax.random.fold_in(_rk, 11), (64, 16, 128), jnp.float32)
        _ctx_1024c = jax.random.dirichlet(jax.random.fold_in(_rk, 511), 0.3 * jnp.ones((16,), jnp.float32), (64, 120))
        _ctx_1024t = jnp.einsum('bsk,bkd->bsd', _ctx_1024c, _ctx_1024P)
        _ctx_1024t = _ctx_1024t * jax.lax.rsqrt(jnp.mean(jnp.square(_ctx_1024t)) + 1e-12) * 0.953939
        ctx_1024 = -1.52775e-05 + 0.999936 * (_ctx_1024t + 0.3 * jax.random.normal(jax.random.fold_in(_rk, 611), (64, 120, 128), jnp.float32))
        return (x, ctx_1024)
    x, ctx_1024 = _rec_inputs()

    def _L0_attn_setup():
        import jax, jax.numpy as jnp
        import numpy as np
        import math
        B, S, HID, H = (2, 256, 128, 16)
        D = HID // H

        def _get_slopes(n):
            start = 2 ** (-2 ** (-(math.log2(n) - 3)))
            return np.array([start * 2 ** (-i) for i in range(n)], dtype=np.float32)
        key = jax.random.key(seed)
        ks = jax.random.split(key, 9)
        sc = 1.0 / math.sqrt(HID)
        return {'x': jax.random.normal(ks[0], (B, S, HID), dtype=jnp.float32), 'Wq': jax.random.normal(ks[1], (HID, HID), dtype=jnp.float32) * sc, 'bq': jnp.zeros((HID,), dtype=jnp.float32), 'Wk': jax.random.normal(ks[2], (HID, HID), dtype=jnp.float32) * sc, 'bk': jnp.zeros((HID,), dtype=jnp.float32), 'Wv': jax.random.normal(ks[3], (HID, HID), dtype=jnp.float32) * sc, 'bv': jnp.zeros((HID,), dtype=jnp.float32), 'Wo': jax.random.normal(ks[4], (HID, HID), dtype=jnp.float32) * sc, 'bo': jnp.zeros((HID,), dtype=jnp.float32), 'slopes': jnp.asarray(_get_slopes(H))}
    _L0_attn_all = _L0_attn_setup()
    _L0_attn_in = {k: v for k, v in _L0_attn_all.items() if k in ('Wq', 'bq', 'Wk', 'bk', 'Wv', 'bv', 'Wo', 'bo', 'slopes')}
    del _L0_attn_all

    def _L0_xattn_setup():
        import jax, jax.numpy as jnp
        import numpy as np
        key = jax.random.key(seed)
        kq, kk, kv = jax.random.split(key, 3)
        bs, s, d = (16, 256, 128)
        return {'query': jax.random.normal(kq, (bs, s, d), dtype=jnp.float32), 'key': jax.random.normal(kk, (bs, s, d), dtype=jnp.float32), 'value': jax.random.normal(kv, (bs, s, d), dtype=jnp.float32)}
    _L0_xattn_all = _L0_xattn_setup()
    _L0_xattn_in = {k: v for k, v in _L0_xattn_all.items() if k in ()}
    del _L0_xattn_all

    def _L0_ffn_setup():
        import jax, jax.numpy as jnp
        import numpy as np
        key = jax.random.key(seed)
        k0, k1, k2, k3 = jax.random.split(key, 4)
        B, S, D, F, E = (8, 256, 128, 256, 8)
        x = jax.random.normal(k0, (B, S, D), dtype=jnp.float32)
        Wg = jax.random.normal(k1, (D, E), dtype=jnp.float32) * 0.02
        W1 = jax.random.normal(k2, (E, D, F), dtype=jnp.float32) * 0.02
        W2 = jax.random.normal(k3, (E, F, D), dtype=jnp.float32) * 0.02
        return {'x': x, 'Wg': Wg, 'W1': W1, 'W2': W2}
    _L0_ffn_all = _L0_ffn_setup()
    _L0_ffn_in = {k: v for k, v in _L0_ffn_all.items() if k in ('Wg', 'W1', 'W2')}
    del _L0_ffn_all
    return {'x': x, 'ctx_1024': ctx_1024, 'L0_attn_Wq': _L0_attn_in['Wq'], 'L0_attn_bq': _L0_attn_in['bq'], 'L0_attn_Wk': _L0_attn_in['Wk'], 'L0_attn_bk': _L0_attn_in['bk'], 'L0_attn_Wv': _L0_attn_in['Wv'], 'L0_attn_bv': _L0_attn_in['bv'], 'L0_attn_Wo': _L0_attn_in['Wo'], 'L0_attn_bo': _L0_attn_in['bo'], 'L0_attn_slopes': _L0_attn_in['slopes'], 'L0_ffn_Wg': _L0_ffn_in['Wg'], 'L0_ffn_W1': _L0_ffn_in['W1'], 'L0_ffn_W2': _L0_ffn_in['W2']}

def reference(x, ctx_1024, L0_attn_Wq, L0_attn_bq, L0_attn_Wk, L0_attn_bk, L0_attn_Wv, L0_attn_bv, L0_attn_Wo, L0_attn_bo, L0_attn_slopes, L0_ffn_Wg, L0_ffn_W1, L0_ffn_W2):
    import jax
    import jax.numpy as jnp

    def _L0_attn_ref(x, Wq, bq, Wk, bk, Wv, bv, Wo, bo, slopes):
        import jax, jax.numpy as jnp
        import numpy as np
        import math
        B, S, HID, H = (2, 256, 128, 16)
        D = HID // H

        def _get_slopes(n):
            start = 2 ** (-2 ** (-(math.log2(n) - 3)))
            return np.array([start * 2 ** (-i) for i in range(n)], dtype=np.float32)
        b, s, hid = x.shape
        h = slopes.shape[0]
        d = hid // h
        q = (x @ Wq.T + bq).reshape(b, s, h, d).transpose(0, 2, 1, 3)
        k = (x @ Wk.T + bk).reshape(b, s, h, d).transpose(0, 2, 1, 3)
        v = (x @ Wv.T + bv).reshape(b, s, h, d).transpose(0, 2, 1, 3)
        scores = jnp.einsum('bhqd,bhkd->bhqk', q, k) / jnp.sqrt(jnp.float32(d))
        pos = jnp.arange(s)
        dist = (pos[None, :] - pos[:, None]).astype(x.dtype)
        scores = scores + slopes[None, :, None, None] * dist[None, None]
        attn = jax.nn.softmax(scores, axis=-1)
        ctx = jnp.einsum('bhqk,bhkd->bhqd', attn, v)
        ctx = ctx.transpose(0, 2, 1, 3).reshape(b, s, hid)
        return ctx @ Wo.T + bo

    def _L0_xattn_ref(query, key, value):
        import jax, jax.numpy as jnp
        import numpy as np
        scale = jnp.asarray(query.shape[-1], query.dtype) ** 0.5
        scores = jnp.einsum('bqd,bkd->bqk', query, key) / scale
        attn = jax.nn.softmax(scores, axis=-1)
        return jnp.einsum('bqk,bkd->bqd', attn, value)

    def _L0_ffn_ref(x, Wg, W1, W2):
        import jax, jax.numpy as jnp
        import numpy as np
        B, S, D = x.shape
        E = Wg.shape[1]
        T = B * S
        cap = max(1, T // E)
        xt = x.reshape(T, D)
        logits = xt @ Wg
        probs = jax.nn.softmax(logits, axis=-1)
        pT = probs.T
        _, top_idx = jax.lax.top_k(pT, cap)
        sel = jnp.zeros((E, T), dtype=bool).at[jnp.arange(E)[:, None], top_idx].set(True)
        masked = jnp.where(sel, pT, -jnp.inf)
        assigned = sel.any(axis=0)
        tok2exp = jnp.where(assigned, jnp.argmax(masked, axis=0), jnp.argmax(pT, axis=0))
        weights = jnp.take_along_axis(probs, tok2exp[:, None], axis=1)[:, 0]
        out = jnp.zeros_like(xt)
        for e in range(E):
            gate = jnp.where(tok2exp == e, weights, 0.0)
            h = jax.nn.gelu(xt @ W1[e], approximate=False) @ W2[e]
            out = out + gate[:, None] * h
        return out.reshape(B, S, D)
    x = _layernorm(x + _L0_attn_ref(x, L0_attn_Wq, L0_attn_bq, L0_attn_Wk, L0_attn_bk, L0_attn_Wv, L0_attn_bv, L0_attn_Wo, L0_attn_bo, L0_attn_slopes), axis=-1)
    x = _layernorm(x + _L0_xattn_ref(x, ctx_1024, ctx_1024), axis=-1)
    x = _layernorm(x + _L0_ffn_ref(x, L0_ffn_Wg, L0_ffn_W1, L0_ffn_W2), axis=-1)
    return x

_drawn_inputs = setup_inputs


def setup_inputs(seed=0):
    import zlib

    import numpy as np

    out = dict(_drawn_inputs(seed))
    spreads = {'L0_attn_bq': (0.0, 0.501),
     'L0_attn_bk': (0.0, 0.8),
     'L0_attn_bv': (0.0, 0.1),
     'L0_attn_bo': (0.0, 0.1)}
    factors = {'L0_ffn_Wg': 8.0, 'L0_ffn_W1': 8.0, 'L0_ffn_W2': 8.0}
    for name, (base, spread) in spreads.items():
        noise = np.random.default_rng([zlib.crc32(name.encode()), seed]).standard_normal(out[name].shape)
        drawn = base * np.exp(spread * noise) if base else spread * noise
        out[name] = jnp.asarray(drawn.astype(out[name].dtype))
    for name, factor in factors.items():
        out[name] = (out[name] * factor).astype(out[name].dtype)
    return out
```

```python
from contextlib import ExitStack

import numpy as np

import concourse.bass as bass
from concourse import mybir

ACT = mybir.ActivationFunctionType
ALU = mybir.AluOpType
AX = mybir.AxisListType
F32 = mybir.dt.float32
BF16 = mybir.dt.bfloat16
I32 = mybir.dt.int32

P = 128
B, S, D = 64, 128, 128
SK = 120
H, HD = 16, 8
NG, NC_ = 4, 4
E, F = 8, 256
T = B * S
CAP = max(1, T // E)
NT = T // P + E
ROW = D + 2
EPS = 1e-5
PROB_BITS = 30
SLOPE_ROW, POS_ROW, MAX_ROW = HD, HD + 1, HD + 2

C_ID, C_TQ, C_TK, C_SAME, C_BELOW, C_TRI = (i * P for i in range(6))
C_DESC = 6 * P
C_TILE = C_DESC + E
C_ONES = C_TILE + NT
C_KONE = C_ONES + P
C_TOK = C_KONE + 1
C_N = C_TOK + T // P


def attention_ffn(nc, x, xt, ctx_in, ctxt, wq, wk, wv, wo, bq, bk, slopes, bv, bo, wg, w1, w2, consts, out):
    st = ExitStack()
    with st:
        def sb(name, shape, dt=F32):
            return st.enter_context(nc.sbuf_tensor(name, shape, dt))

        def bank(name):
            return st.enter_context(nc.psum_tensor(name, [P, 512], F32))

        def sem(name):
            return st.enter_context(nc.semaphore(name))

        sorted_rows = nc.dram_tensor("sorted_rows", [NT * P, ROW], F32, kind="Internal").ap()

        cst = sb("cst", [P, C_N])
        ident = cst[:, C_ID:C_ID + P]
        wq_sb, wk_sb, wo_sb = (sb(n, [P, NC_, P]) for n in ("wq_sb", "wk_sb", "wo_sb"))
        wv_sb, wg_sb = sb("wv_sb", [P, P]), sb("wg_sb", [P, E])
        w1_sb, w2_sb = sb("w1_sb", [P, E, F]), sb("w2_sb", [P, E, 2, D])
        bq_sb, bk_sb, sl_sb = (sb(n, [P, NC_]) for n in ("bq_sb", "bk_sb", "sl_sb"))
        bv_sb, bo_sb = sb("bv_sb", [P, 1]), sb("bo_sb", [1, P])
        q_add, k_add = sb("q_add", [P, NC_, P]), sb("k_add", [P, NC_, P])
        bv_wide, out_bias = sb("bv_wide", [P, P]), sb("out_bias", [P, P])
        tri_bf, ones_bf = sb("tri_bf", [P, P], BF16), sb("ones_bf", [P, P], BF16)
        ones32 = cst[:, C_ONES:C_ONES + 32]
        neg_half, eps = sb("neg_half", [P, 1]), sb("eps", [P, 1])
        blank_row = sb("blank_row", [P, ROW])

        xt_sb = [sb(f"xt_sb{u}", [P, P]) for u in range(2)]
        x_sb = [sb(f"x_sb{u}", [P, P]) for u in range(2)]
        c_sb = [sb(f"c_sb{u}", [SK, P]) for u in range(2)]
        ct_sb = [sb(f"ct_sb{u}", [P, SK]) for u in range(2)]
        x_plus_bias = [sb(f"x_plus_bias{u}", [P, P]) for u in range(2)]
        qt = [sb(f"qt{u}", [P, NC_, P]) for u in range(2)]
        kt = [sb(f"kt{u}", [P, NC_, P]) for u in range(2)]
        v_sb = [sb(f"v_sb{u}", [P, P]) for u in range(2)]
        q_less_max = sb("q_less_max", [P, NC_, P])
        neg_max = sb("neg_max", [P, NC_, P])
        probs_t = sb("probs_t", [P, NG, 512])
        den_rec, heads_out = sb("den_rec", [P, 512]), sb("heads_out", [P, NC_, P])
        t1, x1, t2, x2 = (sb(n, [P, P]) for n in ("t1", "x1", "t2", "x2"))
        x1t, x2t, p2, p2t = sb("x1t", [P, P]), sb("x2t", [P, P]), sb("p2", [P, SK]), sb("p2t", [SK, P])
        stats1, stats2 = sb("stats1", [P, 6]), sb("stats2", [P, 6])
        mv1, mv2 = sb("mv1", [P, 2]), sb("mv2", [P, 2])
        ve1, ve2, rstd1, rstd2 = (sb(n, [P, 1]) for n in ("ve1", "ve2", "rstd1", "rstd2"))
        neg_max2, sum2, rec2 = (sb(n, [P, 1]) for n in ("neg_max2", "sum2", "rec2"))
        rows = sb("rows", [P, B, ROW])

        proj_bank, pv_bank, den_bank, tail_bank = (bank(n) for n in ("proj_bank", "pv_bank", "den_bank", "tail_bank"))
        score_bank = [bank(f"score_bank{g}") for g in range(NG)]
        slot = [tail_bank[:, i * P:(i + 1) * P] for i in range(4)]

        logits = sb("logits", [P, B, E])
        tok_a, tok_b, tok_c, prob = (sb(n, [P, B, E]) for n in ("tok_a", "tok_b", "tok_c", "prob"))
        ro_t, ro_u, weight = sb("ro_t", [P, B]), sb("ro_u", [P, B]), sb("weight", [P, B])
        prob_e, ex_a, ex_b, ex_c = (sb(n, [P, 512]) for n in ("prob_e", "ex_a", "ex_b", "ex_c"))
        thr, cand, keep, cnt, cnt2 = (sb(n, [P, 1]) for n in ("thr", "cand", "keep", "cnt", "cnt2"))
        bit = sb("bit", [P, 1], I32)
        need, before = sb("need", [P, 1]), sb("before", [P, 1])
        onehot_bf = sb("onehot_bf", [P, E, B], BF16)
        e_f = [sb(f"e_f{i}", [P, E]) for i in range(5)]
        e_i, e_i2 = sb("e_i", [P, E], I32), sb("e_i2", [P, E], I32)
        tile_cmp = sb("tile_cmp", [P, NT, E - 1])
        tile_e, tile_ei = sb("tile_e", [P, NT]), sb("tile_ei", [P, NT], I32)
        pos_f = sb("pos_f", [P, B])

        RS = 4
        row_stage = [sb(f"row_stage{i}", [P, ROW]) for i in range(RS)]
        pos_stage = [sb(f"pos_stage{i}", [P, 1], I32) for i in range(RS)]
        xs = [sb(f"xs{i}", [P, ROW]) for i in range(RS)]
        xs_t = [sb(f"xs_t{i}", [P, P]) for i in range(2)]
        hid = [sb(f"hid{i}", [P, F]) for i in range(2)]
        hid_t = sb("hid_t", [P, 2, P])
        y1 = sb("y1", [P, P])
        y2 = [sb(f"y2_{i}", [P, P]) for i in range(RS)]
        tok_i = [sb(f"tok_i{i}", [P, 1], I32) for i in range(RS)]
        stats3, mv3, ve3, rstd3 = sb("stats3", [P, 6]), sb("mv3", [P, 2]), sb("ve3", [P, 1]), sb("rstd3", [P, 1])

        names = """weights_in prep blank_made front_in0 front_in1 back_in0 back_in1 blanks_out
        k_proj q_proj v_proj scored max_turned rescored pv_done projected x1_turned scored2 p2_turned
        attended2 x2_turned gated bias_made
        k_ready q_ready max_ready qm_ready den_ready heads_ready t1_ready st1_ready mv1_ready x1_ready
        max2_ready rec2_ready t2_ready st2_ready mv2_ready x2_ready logits_ready
        x1t_ready p2_ready v_ready p2t_ready probs_ready x2t_ready
        xb_ready ve1_ready rstd1_ready ve2_ready rstd2_ready row_kept
        dve_step gate_max_ready gate_exp gates_turned counted sel_turned ranked found searched bit_ready
        table_ready staged0 staged1 staged2 staged3 scattered0 scattered1 scattered2 scattered3 xs_in0 xs_in1 xs_in2 xs_in3
        xs_turned xs_t_ready hid_made hid_ready hid_turned hid_t_ready y_made y1_ready st3_ready mv3_ready ve3_ready
        rstd3_ready y2_ready tok_ready out_stored0 out_stored1 out_stored2 out_stored3""".split()
        s = {n: sem(n) for n in names}
        (weights_in, prep, blank_made, front_in0, front_in1, back_in0, back_in1, blanks_out,
         k_proj, q_proj, v_proj, scored, max_turned, rescored, pv_done, projected, x1_turned, scored2, p2_turned,
         attended2, x2_turned, gated, bias_made,
         k_ready, q_ready, max_ready, qm_ready, den_ready, heads_ready, t1_ready, st1_ready, mv1_ready, x1_ready,
         max2_ready, rec2_ready, t2_ready, st2_ready, mv2_ready, x2_ready, logits_ready,
         x1t_ready, p2_ready, v_ready, p2t_ready, probs_ready, x2t_ready,
         xb_ready, ve1_ready, rstd1_ready, ve2_ready, rstd2_ready, row_kept,
         dve_step, gate_max_ready, gate_exp, gates_turned, counted, sel_turned, ranked, found, searched, bit_ready,
         table_ready, staged0, staged1, staged2, staged3, scattered0, scattered1, scattered2, scattered3,
         xs_in0, xs_in1, xs_in2, xs_in3,
         xs_turned, xs_t_ready, hid_made, hid_ready, hid_turned, hid_t_ready, y_made, y1_ready, st3_ready, mv3_ready,
         ve3_ready, rstd3_ready, y2_ready, tok_ready, out_stored0, out_stored1, out_stored2,
         out_stored3) = (s[n] for n in names)
        front_in, back_in = [front_in0, front_in1], [back_in0, back_in1]
        staged = [staged0, staged1, staged2, staged3]
        scattered = [scattered0, scattered1, scattered2, scattered3]
        xs_in = [xs_in0, xs_in1, xs_in2, xs_in3]
        out_stored = [out_stored0, out_stored1, out_stored2, out_stored3]
        N_WEIGHTS = 15 * 16

        def ge(eng, semaphore, value):
            if not (isinstance(value, int) and value <= 0):
                eng.wait_ge(semaphore, value)

        def alone(eng):
            eng.wait_ge(weights_in, N_WEIGHTS)

        def batches(eng, step):
            step(0, 0, lambda d: d // 2, True, False)
            with eng.Fori(0, (B - 2) // 2) as i:
                for u in range(2):
                    step(i * 2 + (1 + u), (1 + u) % 2, lambda d: i + (1 + u + d) // 2, False, False)
            step(B - 1, (B - 1) % 2, lambda d: (B - 1 + d) // 2, False, True)

        def tiles(eng, step):
            lead = RS + 1
            for j in range(lead):
                step(j, j % RS, lambda d: (j + d) // RS, j == 0, False)
            n = (NT - 1 - lead) // RS
            with eng.Fori(0, n) as i:
                for u in range(RS):
                    step(i * RS + (lead + u), (lead + u) % RS, lambda d: i + (lead + u + d) // RS, False, False)
            for j in range(lead + n * RS, NT):
                step(j, j % RS, lambda d: (j + d) // RS, False, j == NT - 1)

        block = st.enter_context(nc.Block())

        @block.sync
        def _(sp):
            def front(n, u):
                sp.dma_start(xt_sb[u][:, :], xt[n]).then_inc(front_in[u], 16)

            def back(n, u):
                sp.dma_start(x_sb[u][:, :], x[n]).then_inc(back_in[u], 16)
                sp.dma_start(c_sb[u][:, :], ctx_in[n]).then_inc(back_in[u], 16)
                sp.dma_start(ct_sb[u][:, :], ctxt[n]).then_inc(back_in[u], 16)

            front(0, 0)
            front(1, 1)
            back(0, 0)
            back(1, 1)
            sp.wait_ge(q_proj, 1)
            front(2, 0)
            with sp.Fori(0, (B - 4) // 2) as i:
                for v in range(2):
                    b, u = i * 2 + (1 + v), (1 + v) % 2
                    sp.wait_ge(q_proj, b + 1)
                    front(b + 2, u)
                    sp.wait_ge(attended2, b)
                    sp.wait_ge(xb_ready, b)
                    back(b + 1, 1 - u)
            for b in (B - 3, B - 2):
                if b + 2 < B:
                    sp.wait_ge(q_proj, b + 1)
                    front(b + 2, b % 2)
                sp.wait_ge(attended2, b)
                sp.wait_ge(xb_ready, b)
                back(b + 1, (b + 1) % 2)

            for r in range(RS):
                sp.wait_ge(scattered[r], 16 * (B // RS))

            def load_rows(j, u):
                sp.dma_start(xs[u][:, :], sorted_rows[bass.ts(j, P), :]).then_inc(xs_in[u], 16)

            for j in range(RS):
                load_rows(j, j)
            with sp.Fori(0, NT // RS - 1) as i:
                for u in range(RS):
                    j = i * RS + u
                    sp.wait_ge(y1_ready, j + 1)
                    sp.wait_ge(tok_ready, j + 1)
                    load_rows(j + RS, u)

        @block.tensor
        def _(pe):
            def project_k(n, u, loads):
                pe.wait_ge(front_in[u], loads * 16)
                ge(pe, q_ready, n)
                for c in range(NC_):
                    mm = pe.matmul(proj_bank[:, c * P:(c + 1) * P], wk_sb[:, c, :], xt_sb[u][:, :], start=True, stop=True)
                mm.then_inc(k_proj, 1)

            def project_v(n, u):
                ge(pe, v_ready, n)
                pe.matmul(den_bank[:, 0:P], xt_sb[u][:, :], wv_sb[:, :], start=True, stop=True).then_inc(v_proj, 1)

            def project_q(n, u):
                if isinstance(n, int) and n == 0:
                    pe.wait_ge(k_ready, 1)
                else:
                    pe.wait_ge(qm_ready, n)
                for c in range(NC_):
                    mm = pe.matmul(proj_bank[:, c * P:(c + 1) * P], wq_sb[:, c, :], xt_sb[u][:, :], start=True, stop=True)
                mm.then_inc(q_proj, 1)

            def score(b, u, g):
                if g == 0:
                    pe.wait_ge(k_ready, b + 1)
                    pe.wait_ge(q_ready, b + 1)
                ge(pe, probs_ready, 4 * b + g - 3)
                r = slice(32 * g, 32 * g + 32)
                for c in range(NC_):
                    mm = pe.matmul(score_bank[g][:, c * P:(c + 1) * P], qt[u][r, c, :], kt[u][r, c, :],
                                   start=True, stop=True, tile_position=(32 * g, 0))
                mm.then_inc(scored, 1)

            def turn_max(b, last):
                pe.wait_ge(max_ready, 4 * b + 4)
                if not last:
                    pe.wait_ge(k_ready, b + 2)
                for c in range(NC_):
                    mm = pe.transpose(proj_bank[:, c * P:(c + 1) * P], neg_max[:, c, :], ident)
                mm.then_inc(max_turned, 1)

            def rescore(b, u, g):
                if g == 0:
                    pe.wait_ge(qm_ready, b + 1)
                r = slice(32 * g, 32 * g + 32)
                for c in range(NC_):
                    mm = pe.matmul(score_bank[g][:, c * P:(c + 1) * P], kt[u][r, c, :], q_less_max[r, c, :],
                                   start=True, stop=True, tile_position=(32 * g, 0))
                mm.then_inc(rescored, 1)

            def values(b, u, g, values_kept=0):
                if g == 0:
                    ge(pe, heads_ready, b)
                    pe.wait_ge(v_ready, values_kept)
                pe.wait_ge(probs_ready, 4 * b + g + 1)
                r = slice(32 * g, 32 * g + 32)
                pe.matmul(pv_bank[r, :], v_sb[u][:, r], probs_t[:, g, :], start=True, stop=True,
                          tile_position=(0, 32 * g))
                pe.matmul(den_bank[r, :], ones32, probs_t[:, g, :], start=True, stop=True,
                          tile_position=(0, 32 * g)).then_inc(pv_done, 1)

            def project_out(p):
                pe.wait_ge(heads_ready, p + 1)
                for c in range(NC_):
                    mm = pe.matmul(slot[0], heads_out[:, c, :], wo_sb[:, c, :], start=(c == 0), stop=(c == NC_ - 1))
                mm.then_inc(projected, 1)

            def turn_x1(p):
                pe.wait_ge(x1_ready, p + 1)
                pe.transpose(slot[1], x1[:, :], ident).then_inc(x1_turned, 1)

            def score2(p, u, loads):
                pe.wait_ge(back_in[u], loads * 48)
                pe.wait_ge(x1t_ready, p + 1)
                pe.matmul(slot[2][:, 0:SK], x1t[:, :], ct_sb[u][:, :], start=True, stop=True).then_inc(scored2, 1)

            def turn_p2(p):
                pe.wait_ge(p2_ready, p + 1)
                pe.transpose(slot[3][0:SK, :], p2[:, :], ident).then_inc(p2_turned, 1)

            def attend2(p, u):
                pe.wait_ge(p2t_ready, p + 1)
                pe.wait_ge(t1_ready, p + 1)
                pe.matmul(slot[0], p2t[:, :], c_sb[u][:, :], start=True, stop=True).then_inc(attended2, 1)

            def turn_x2(p):
                pe.wait_ge(x2_ready, p + 1)
                pe.transpose(slot[1], x2[:, :], ident).then_inc(x2_turned, 1)

            def gate(p):
                pe.wait_ge(x2t_ready, p + 1)
                pe.wait_ge(p2_ready, p + 1)
                pe.matmul(slot[2][:, 0:E], x2t[:, :], wg_sb[:, :], start=True, stop=True).then_inc(gated, 1)

            pe.wait_ge(weights_in, N_WEIGHTS)
            pe.wait_ge(prep, 1)
            for c in range(NC_):
                pe.matmul(slot[0], bv_wide[:, :], wo_sb[:, c, :], start=(c == 0), stop=False)
            pe.matmul(slot[0], cst[0:1, C_ONES:C_ONES + P], bo_sb[:, :], start=False, stop=True).then_inc(bias_made, 1)
            pe.wait_ge(prep, 2)
            project_k(0, 0, 1)
            project_v(0, 0)
            project_q(0, 0)

            def step(b, u, half, first, last):
                p, n = b - 1, b + 1
                score(b, u, 0)
                if not first:
                    project_out(p)
                score(b, u, 1)
                if not last:
                    project_k(n, 1 - u, half(1) + 1)
                    project_v(n, 1 - u)
                score(b, u, 2)
                if not first:
                    turn_x1(p)
                score(b, u, 3)
                if not first:
                    score2(p, 1 - u, half(-1) + 1)
                turn_max(b, last)
                if not first:
                    turn_p2(p)
                rescore(b, u, 0)
                if not first:
                    attend2(p, 1 - u)
                rescore(b, u, 1)
                values(b, u, 0, b + 1 if last else b + 2)
                if not last:
                    project_q(n, 1 - u)
                if not first:
                    turn_x2(p)
                rescore(b, u, 2)
                values(b, u, 1)
                if not first:
                    gate(p)
                rescore(b, u, 3)
                values(b, u, 2)
                values(b, u, 3)

            batches(pe, step)
            p, u = B - 1, (B - 1) % 2
            project_out(p)
            turn_x1(p)
            score2(p, u, B // 2)
            turn_p2(p)
            attend2(p, u)
            turn_x2(p)
            gate(p)

            pe.wait_ge(found, 1)
            for b4 in range(4):
                mm = pe.transpose(score_bank[0][:, b4 * P:(b4 + 1) * P], ex_b[:, b4 * P:(b4 + 1) * P], ident)
            mm.then_inc(gates_turned, 1)

            def count(n, rhs, weights, dst):
                pe.wait_ge(searched, n)
                pe.matmul(dst, weights, rhs, start=True, stop=True).then_inc(counted, 1)

            same = cst[:, C_SAME:C_SAME + P]
            with pe.Fori(0, PROB_BITS) as i:
                count(i + 1, cnt[:, :], same, score_bank[1][:, 0:1])
            count(PROB_BITS + 1, cnt[:, :], same, score_bank[1][:, 0:1])
            count(PROB_BITS + 2, cnt2[:, :], cst[:, C_BELOW:C_BELOW + P], score_bank[1][:, 1:2])
            pe.wait_ge(found, 2)
            for b4 in range(4):
                mm = pe.transpose(score_bank[0][:, b4 * P:(b4 + 1) * P], ex_a[:, b4 * P:(b4 + 1) * P], ident)
            mm.then_inc(sel_turned, 1)
            pe.wait_ge(found, 3)
            pe.matmul(score_bank[1][:, :], tri_bf[:, :], onehot_bf[:, :, :], start=True, stop=True)
            pe.matmul(score_bank[2][:, :], ones_bf[:, :], onehot_bf[:, :, :], start=True, stop=True).then_inc(ranked, 1)

            y_bank = [den_bank, proj_bank]
            h_bank = [score_bank[2], score_bank[3]]

            def turn_rows(j, u4, loads):
                pe.wait_ge(xs_in[u4], loads * 16)
                pe.transpose(score_bank[0][:, 0:P], xs[u4][:, 0:D], ident).then_inc(xs_turned, 1)

            def hidden(j, u2):
                e = pe.value_load(tile_ei[0:1, bass.ds(j, 1)], min_val=0, max_val=E - 1)
                pe.wait_ge(xs_t_ready, j + 1)
                pe.matmul(h_bank[u2][:, 0:F], xs_t[u2][:, :], w1_sb[:, e, :], start=True, stop=True).then_inc(hid_made, 1)

            def turn_hidden(j, u2):
                pe.wait_ge(hid_ready, j + 1)
                pe.transpose(pv_bank[:, 0:P], hid[u2][:, 0:P], ident)
                pe.transpose(pv_bank[:, P:2 * P], hid[u2][:, P:2 * P], ident).then_inc(hid_turned, 1)

            def back_to_rows(j, u2):
                e = pe.value_load(tile_ei[0:1, bass.ds(j, 1)], min_val=0, max_val=E - 1)
                pe.wait_ge(hid_t_ready, j + 1)
                pe.matmul(y_bank[u2][:, 0:D], hid_t[:, 0, :], w2_sb[:, e, 0, :], start=True, stop=False)
                pe.matmul(y_bank[u2][:, 0:D], hid_t[:, 1, :], w2_sb[:, e, 1, :], start=False, stop=True).then_inc(y_made, 1)

            pe.wait_ge(table_ready, 1)
            turn_rows(0, 0, 1)

            def ffn(j, u4, turn, first, last):
                u2 = u4 % 2
                hidden(j, u2)
                if not first:
                    turn_hidden(j - 1, 1 - u2)
                if not last:
                    turn_rows(j + 1, (u4 + 1) % RS, turn(1) + 1)
                if not first:
                    back_to_rows(j - 1, 1 - u2)

            tiles(pe, ffn)
            turn_hidden(NT - 1, (NT - 1) % 2)
            back_to_rows(NT - 1, (NT - 1) % 2)

        @block.vector
        def _(dve):
            steps = [0]

            def then(ins):
                steps[0] += 1
                ins.then_inc(dve_step, 1)
                dve.wait_ge(dve_step, steps[0])

            then(dve.memset(neg_max[:, :, :], 0.0))
            dve.wait_ge(weights_in, N_WEIGHTS)
            then(dve.memset(bv_wide[:, :], 0.0))
            dve.tensor_scalar(bv_wide[:, :], bv_wide[:, :], bv_sb[:, 0:1], None, ALU.add).then_inc(prep, 1)
            then(dve.tensor_scalar(bq_sb[:, :], bq_sb[:, :], HD ** -0.5, None, ALU.mult))
            then(dve.tensor_tensor(bq_sb[:, :], bq_sb[:, :], sl_sb[:, :], ALU.add))
            then(dve.tensor_scalar(bk_sb[:, :], bk_sb[:, :], cst[:, C_KONE:C_KONE + 1], None, ALU.add))
            for c in range(NC_):
                then(dve.tensor_scalar(q_add[:, c, :], cst[:, C_TQ:C_TQ + P], bq_sb[:, c:c + 1], None, ALU.mult))
                then(dve.tensor_scalar(k_add[:, c, :], cst[:, C_TK:C_TK + P], bk_sb[:, c:c + 1], None, ALU.mult))
            then(dve.tensor_copy(tri_bf[:, :], cst[:, C_TRI:C_TRI + P]))
            then(dve.memset(ones_bf[:, :], 1.0))
            dve.tensor_scalar(wq_sb[:, :, :], wq_sb[:, :, :], HD ** -0.5, None, ALU.mult).then_inc(prep, 1)
            dve.wait_ge(bias_made, 1)
            dve.tensor_copy(out_bias[:, :], slot[0]).then_inc(prep, 1)

            def k_rows(n, u):
                dve.wait_ge(k_proj, n + 1)
                dve.tensor_tensor(kt[u][:, :, :], proj_bank[:, :].rearrange("p (c t) -> p c t", c=NC_), k_add[:, :, :],
                                  ALU.add).then_inc(k_ready, 1)

            def q_rows(n, u):
                dve.wait_ge(q_proj, n + 1)
                dve.tensor_tensor(qt[u][:, :, :], proj_bank[:, :].rearrange("p (c t) -> p c t", c=NC_), q_add[:, :, :],
                                  ALU.add).then_inc(q_ready, 1)

            def row_max(b, g):
                dve.wait_ge(scored, 4 * b + g + 1)
                if g == 0:
                    ge(dve, max_turned, b)
                dve.tensor_reduce(neg_max[:, :, 32 * g + MAX_ROW], score_bank[g][:, :].rearrange("p (c k) -> p c k", c=NC_),
                                  AX.X, ALU.max, negate=True).then_inc(max_ready, 1)

            def q_with_max(b, u):
                dve.wait_ge(max_turned, b + 1)
                dve.tensor_tensor(q_less_max[:, :, :], proj_bank[:, :].rearrange("p (c t) -> p c t", c=NC_),
                                  qt[u][:, :, :], ALU.add).then_inc(qm_ready, 1)

            def normalise(b):
                dve.wait_ge(pv_done, 4 * b + 4)
                dve.reciprocal(den_rec[:, :], den_bank[:, :]).then_inc(den_ready, 1)
                dve.wait_ge(den_ready, b + 1)
                dve.tensor_tensor(heads_out[:, :, :], pv_bank[:, :].rearrange("p (c t) -> p c t", c=NC_),
                                  den_rec[:, :].rearrange("p (c t) -> p c t", c=NC_), ALU.mult).then_inc(heads_ready, 1)

            def residual1(p, u):
                dve.wait_ge(projected, p + 1)
                dve.wait_ge(xb_ready, p + 1)
                dve.tensor_tensor(t1[:, :], slot[0], x_plus_bias[u][:, :], ALU.add).then_inc(t1_ready, 1)
                dve.wait_ge(t1_ready, p + 1)
                dve.bn_stats(stats1[:, :], t1[:, :]).then_inc(st1_ready, 1)
                alone(dve)
                dve.wait_ge(st1_ready, p + 1)
                dve.bn_aggr(mv1[:, :], stats1[:, :]).then_inc(mv1_ready, 1)

            def norm1(p):
                dve.wait_ge(rstd1_ready, p + 1)
                dve.tensor_scalar(x1[:, :], t1[:, :], mv1[:, 0:1], rstd1[:, 0:1], ALU.subtract,
                                  ALU.mult).then_inc(x1_ready, 1)

            def row_max2(p):
                dve.wait_ge(scored2, p + 1)
                dve.tensor_reduce(neg_max2[:, :], slot[2][:, 0:SK], AX.X, ALU.max, negate=True).then_inc(max2_ready, 1)

            def residual2(p):
                dve.wait_ge(p2_ready, p + 1)
                dve.reciprocal(rec2[:, :], sum2[:, :]).then_inc(rec2_ready, 1)
                dve.wait_ge(rec2_ready, p + 1)
                dve.wait_ge(attended2, p + 1)
                dve.scalar_tensor_tensor(t2[:, :], slot[0], rec2[:, 0:1], x1[:, :], ALU.mult,
                                         ALU.add).then_inc(t2_ready, 1)
                dve.wait_ge(t2_ready, p + 1)
                dve.bn_stats(stats2[:, :], t2[:, :]).then_inc(st2_ready, 1)
                alone(dve)
                dve.wait_ge(st2_ready, p + 1)
                dve.bn_aggr(mv2[:, :], stats2[:, :]).then_inc(mv2_ready, 1)

            def norm2(p):
                dve.wait_ge(rstd2_ready, p + 1)
                dve.tensor_scalar(x2[:, :], t2[:, :], mv2[:, 0:1], rstd2[:, 0:1], ALU.subtract,
                                  ALU.mult).then_inc(x2_ready, 1)

            def keep_logits(p):
                dve.wait_ge(gated, p + 1)
                dve.tensor_copy(logits[:, p, :], slot[2][:, 0:E]).then_inc(logits_ready, 1)

            k_rows(0, 0)
            q_rows(0, 0)

            def step(b, u, half, first, last):
                p, n = b - 1, b + 1
                row_max(b, 0)
                if not first:
                    residual1(p, 1 - u)
                row_max(b, 1)
                if not last:
                    k_rows(n, 1 - u)
                row_max(b, 2)
                if not first:
                    norm1(p)
                row_max(b, 3)
                if not first:
                    row_max2(p)
                q_with_max(b, u)
                if not first:
                    residual2(p)
                if not last:
                    q_rows(n, 1 - u)
                if not first:
                    norm2(p)
                    keep_logits(p)
                normalise(b)

            batches(dve, step)
            p, u = B - 1, (B - 1) % 2
            residual1(p, u)
            norm1(p)
            row_max2(p)
            residual2(p)
            norm2(p)
            keep_logits(p)

            def over_e(a):
                return a.unsqueeze(2).broadcast_to([P, B, E])

            dve.wait_ge(logits_ready, B)
            then(dve.tensor_reduce(ro_t[:, :], logits[:, :, :], AX.X, ALU.max))
            dve.tensor_tensor(tok_a[:, :, :], logits[:, :, :], over_e(ro_t[:, :]), ALU.subtract).then_inc(gate_max_ready, 1)
            dve.wait_ge(gate_exp, 1)
            then(dve.tensor_reduce(ro_t[:, :], tok_b[:, :, :], AX.X, ALU.add))
            then(dve.reciprocal(ro_u[:, :], ro_t[:, :]))
            then(dve.tensor_tensor(prob[:, :, :], tok_b[:, :, :], over_e(ro_u[:, :]), ALU.mult))
            dve.tensor_copy(ex_b[:, :].rearrange("p (b i e) -> p b i e", b=4, e=E),
                            prob[:, :, :].rearrange("p (i b) e -> p b i e", b=4)).then_inc(found, 1)

            then(dve.memset(thr[:, :], 0.0))
            then(dve.memset(bit[:, :], 1 << (PROB_BITS - 1)))
            dve.wait_ge(gates_turned, 1)
            then(dve.tensor_copy(prob_e[:, :], score_bank[0][:, :]))
            base = steps[0]
            with dve.Fori(0, PROB_BITS) as i:
                dve.tensor_tensor(cand[:, :].bitcast(I32), thr[:, :].bitcast(I32), bit[:, :],
                                  ALU.bitwise_or).then_inc(dve_step, 1)
                dve.wait_ge(dve_step, i * 4 + (base + 1))
                dve.tensor_scalar(ex_a[:, :], prob_e[:, :], cand[:, 0:1], None, ALU.is_ge, ALU.add,
                                  accum_out=cnt[:, :]).then_inc(searched, 1)
                dve.tensor_scalar(bit[:, :], bit[:, :], 1, None, ALU.logical_shift_right).then_inc(dve_step, 1)
                dve.wait_ge(counted, i + 1)
                dve.tensor_scalar(keep[:, :], score_bank[1][:, 0:1], float(CAP), cand[:, 0:1], ALU.is_ge,
                                  ALU.mult).then_inc(dve_step, 1)
                dve.wait_ge(dve_step, i * 4 + (base + 3))
                dve.tensor_tensor(thr[:, :], thr[:, :], keep[:, :], ALU.max).then_inc(dve_step, 1)
                dve.wait_ge(dve_step, i * 4 + (base + 4))
            steps[0] += 4 * PROB_BITS

            dve.tensor_scalar(ex_a[:, :], prob_e[:, :], thr[:, 0:1], None, ALU.is_gt, ALU.add,
                              accum_out=cnt[:, :]).then_inc(searched, 1)
            dve.tensor_scalar(ex_b[:, :], prob_e[:, :], thr[:, 0:1], None, ALU.is_equal, ALU.add,
                              accum_out=cnt2[:, :]).then_inc(searched, 1)
            dve.wait_ge(searched, PROB_BITS + 2)
            then(dve.tensor_tensor_scan(ex_c[:, :], cst[:, C_ONES:C_ONES + 1].broadcast_to([P, 512]),
                                        ex_b[:, :], 0.0, ALU.mult, ALU.add))
            dve.wait_ge(counted, PROB_BITS + 2)
            then(dve.tensor_scalar(need[:, :], score_bank[1][:, 0:1], -1.0, float(CAP), ALU.mult, ALU.add))
            then(dve.tensor_copy(before[:, :], score_bank[1][:, 1:2]))
            then(dve.tensor_scalar(ex_c[:, :], ex_c[:, :], before[:, 0:1], need[:, 0:1], ALU.add, ALU.is_le))
            then(dve.tensor_tensor(ex_c[:, :], ex_c[:, :], ex_b[:, :], ALU.mult))
            dve.tensor_tensor(ex_a[:, :], ex_a[:, :], ex_c[:, :], ALU.add).then_inc(found, 1)

            dve.wait_ge(sel_turned, 1)
            sel = tok_a
            sv = sel[:, :, :].rearrange("p (i b) e -> p b i e", b=4)
            kb = score_bank[0][:, :].rearrange("p (b i e) -> p b i e", b=4, e=E)
            then(dve.tensor_copy(sv, kb))
            then(dve.tensor_tensor(tok_b[:, :, :], prob[:, :, :], sel[:, :, :], ALU.mult))
            then(dve.scalar_tensor_tensor(tok_b[:, :, :], sel[:, :, :], -1.0, tok_b[:, :, :], ALU.add, ALU.add))
            then(dve.tensor_reduce(ro_t[:, :], tok_b[:, :, :], AX.X, ALU.max))
            then(dve.tensor_scalar(ro_u[:, :], ro_t[:, :], 0.0, None, ALU.is_lt))
            then(dve.tensor_tensor(tok_c[:, :, :], prob[:, :, :], over_e(ro_u[:, :]), ALU.mult))
            then(dve.tensor_scalar(ro_u[:, :], ro_u[:, :], -1.0, None, ALU.add))
            then(dve.tensor_tensor(tok_c[:, :, :], tok_c[:, :, :], over_e(ro_u[:, :]), ALU.add))
            then(dve.tensor_tensor(tok_b[:, :, :], tok_b[:, :, :], tok_c[:, :, :], ALU.max))
            then(dve.tensor_reduce(weight[:, :], tok_b[:, :, :], AX.X, ALU.max))
            then(dve.tensor_tensor(tok_b[:, :, :], tok_b[:, :, :], over_e(weight[:, :]), ALU.is_equal))
            desc = cst[:, C_DESC:C_DESC + E].unsqueeze(1).broadcast_to([P, B, E])
            then(dve.tensor_tensor(tok_b[:, :, :], tok_b[:, :, :], desc, ALU.mult))
            then(dve.tensor_reduce(ro_t[:, :], tok_b[:, :, :], AX.X, ALU.max))
            onehot = tok_c
            then(dve.tensor_tensor(onehot[:, :, :], tok_b[:, :, :], over_e(ro_t[:, :]), ALU.is_equal))
            dve.tensor_copy(onehot_bf[:, :, :], onehot[:, :, :].rearrange("p t e -> p e t")).then_inc(found, 1)

            dve.wait_ge(ranked, 1)
            ends, totals = ex_b, ex_a
            then(dve.tensor_copy(totals[:, :], score_bank[2][:, :]))
            then(dve.tensor_tensor_scan(ends[:, :], cst[:, C_ONES:C_ONES + 1].broadcast_to([P, 512]),
                                        totals[:, :], 0.0, ALU.mult, ALU.add))
            then(dve.tensor_tensor(totals[:, :], ends[:, :], totals[:, :], ALU.subtract))
            start_e = totals[:, :].rearrange("p (e t) -> p e t", e=E)[:, :, 0]
            end_e = ends[:, :].rearrange("p (e t) -> p e t", e=E)[:, :, B - 1]
            then(dve.tensor_tensor(e_f[0][:, :], end_e, start_e, ALU.subtract))
            then(dve.tensor_scalar(e_f[0][:, :], e_f[0][:, :], float(P - 1), None, ALU.add))
            then(dve.tensor_copy(e_i[:, :], e_f[0][:, :]))
            then(dve.tensor_scalar(e_i2[:, :], e_i[:, :], 7, None, ALU.logical_shift_right))
            then(dve.tensor_copy(e_f[1][:, :], e_i2[:, :]))
            then(dve.tensor_tensor_scan(e_f[2][:, :], cst[:, C_ONES:C_ONES + E], e_f[1][:, :], 0.0,
                                        ALU.mult, ALU.add))
            then(dve.tensor_tensor(e_f[3][:, :], e_f[2][:, :], e_f[1][:, :], ALU.subtract))
            then(dve.scalar_tensor_tensor(e_f[4][:, :], e_f[3][:, :], float(P), start_e, ALU.mult, ALU.subtract))
            then(dve.tensor_tensor(tile_cmp[:, :, :],
                                   cst[:, C_TILE:C_TILE + NT].unsqueeze(2).broadcast_to([P, NT, E - 1]),
                                   e_f[2][:, 0:E - 1].unsqueeze(1).broadcast_to([P, NT, E - 1]), ALU.is_ge))
            then(dve.tensor_reduce(tile_e[:, :], tile_cmp[:, :, :], AX.X, ALU.add))
            dve.tensor_copy(tile_ei[:, :], tile_e[:, :]).then_inc(table_ready, 1)
            then(dve.tensor_tensor(totals[:, :], score_bank[1][:, :], totals[:, :], ALU.add))
            slots = ex_c[:, :].rearrange("p (e t) -> p e t", e=E)
            then(dve.tensor_tensor(slots, totals[:, :].rearrange("p (e t) -> p e t", e=E),
                                   e_f[4][:, :].unsqueeze(2).broadcast_to([P, E, B]), ALU.add))
            then(dve.tensor_tensor(tok_a[:, :, :], slots.rearrange("p e t -> p t e"), onehot[:, :, :], ALU.mult))
            then(dve.tensor_reduce(pos_f[:, :], tok_a[:, :, :], AX.X, ALU.add))
            dve.wait_ge(row_kept, B)
            then(dve.tensor_copy(rows[:, :, D], weight[:, :]))
            then(dve.tensor_copy(rows[:, :, D + 1], cst[:, C_TOK:C_TOK + B]))

            def stage(t, r):
                dve.tensor_copy(row_stage[r][:, :], rows[:, t, :]).then_inc(staged[r], 1)
                dve.tensor_copy(pos_stage[r][:, :], pos_f[:, bass.ds(t, 1)]).then_inc(staged[r], 1)

            for t in range(RS):
                stage(t, t)
            with dve.Fori(1, B // RS) as i:
                for r in range(RS):
                    dve.wait_ge(scattered[r], i * 16)
                    stage(i * RS + r, r)

            def hidden_rows(j):
                dve.wait_ge(hid_turned, j + 1)
                dve.tensor_copy(hid_t[:, :, :], pv_bank[:, 0:F].rearrange("p (c t) -> p c t", c=2)).then_inc(hid_t_ready, 1)

            def ffn_norm(j, u4, stores):
                dve.wait_ge(y_made, j + 1)
                dve.scalar_tensor_tensor(y1[:, :], [den_bank, proj_bank][u4 % 2][:, 0:D], xs[u4][:, D:D + 1], xs[u4][:, 0:D], ALU.mult,
                                         ALU.add).then_inc(y1_ready, 1)
                ge(dve, out_stored[u4], stores * 16)
                dve.tensor_copy(tok_i[u4][:, :], xs[u4][:, D + 1:D + 2]).then_inc(tok_ready, 1)
                dve.wait_ge(y1_ready, j + 1)
                dve.bn_stats(stats3[:, :], y1[:, :]).then_inc(st3_ready, 1)
                alone(dve)
                dve.wait_ge(st3_ready, j + 1)
                dve.bn_aggr(mv3[:, :], stats3[:, :]).then_inc(mv3_ready, 1)
                dve.wait_ge(rstd3_ready, j + 1)
                dve.tensor_scalar(y2[u4][:, :], y1[:, :], mv3[:, 0:1], rstd3[:, 0:1], ALU.subtract,
                                  ALU.mult).then_inc(y2_ready, 1)

            def ffn(j, u4, turn, first, last):
                if not first:
                    hidden_rows(j - 1)
                    ffn_norm(j - 1, (u4 - 1) % RS, turn(-1))

            tiles(dve, ffn)
            hidden_rows(NT - 1)
            ffn_norm(NT - 1, (NT - 1) % RS, (NT - 1) // RS)

        @block.scalar
        def _(act):
            for dst, src in ((cst[:, :], consts), (wq_sb[:, :, :], wq), (wk_sb[:, :, :], wk), (wv_sb[:, :], wv),
                             (wo_sb[:, :, :], wo), (bq_sb[:, :], bq), (bk_sb[:, :], bk), (sl_sb[:, :], slopes),
                             (bv_sb[:, :], bv), (bo_sb[:, :], bo), (wg_sb[:, :], wg),
                             (w1_sb[:, 0:4, :], w1[0:4].rearrange("e d f -> d e f")),
                             (w1_sb[:, 4:8, :], w1[4:8].rearrange("e d f -> d e f")),
                             (w2_sb[:, :, 0, :], w2[:, 0:P, :].rearrange("e f d -> f e d")),
                             (w2_sb[:, :, 1, :], w2[:, P:F, :].rearrange("e f d -> f e d"))):
                act.dma_start(dst, src).then_inc(weights_in, 16)

            def keep_v(n, u):
                act.wait_ge(v_proj, n + 1)
                nc.scalar.activation(v_sb[u][:, :], den_bank[:, 0:P], ACT.Copy).then_inc(v_ready, 1)

            def keep_x1t(p):
                act.wait_ge(x1_turned, p + 1)
                nc.scalar.activation(x1t[:, :], slot[1], ACT.Copy, scale=D ** -0.5).then_inc(x1t_ready, 1)

            def exp2(p):
                act.wait_ge(max2_ready, p + 1)
                nc.scalar.activation(p2[:, :], slot[2][:, 0:SK], ACT.Exp, bias=neg_max2[:, 0:1],
                                     accum_out=sum2[:, :]).then_inc(p2_ready, 1)

            def keep_p2t(p):
                act.wait_ge(p2_turned, p + 1)
                nc.scalar.activation(p2t[:, :], slot[3][0:SK, :], ACT.Copy).then_inc(p2t_ready, 1)

            def exp(b, g):
                act.wait_ge(rescored, 4 * b + g + 1)
                nc.scalar.activation(probs_t[:, g, :], score_bank[g][:, :], ACT.Exp).then_inc(probs_ready, 1)

            def keep_x2t(p):
                act.wait_ge(x2_turned, p + 1)
                nc.scalar.activation(x2t[:, :], slot[1], ACT.Copy).then_inc(x2t_ready, 1)

            keep_v(0, 0)

            def step(b, u, half, first, last):
                p, n = b - 1, b + 1
                if not last:
                    keep_v(n, 1 - u)
                if not first:
                    keep_x1t(p)
                    exp2(p)
                    keep_p2t(p)
                exp(b, 0)
                exp(b, 1)
                if not first:
                    keep_x2t(p)
                exp(b, 2)
                exp(b, 3)

            batches(act, step)
            p = B - 1
            keep_x1t(p)
            exp2(p)
            keep_p2t(p)
            keep_x2t(p)

            act.wait_ge(gate_max_ready, 1)
            nc.scalar.activation(tok_b[:, :, :], tok_a[:, :, :], ACT.Exp).then_inc(gate_exp, 1)

            def keep_rows_t(j, u2):
                act.wait_ge(xs_turned, j + 1)
                nc.scalar.activation(xs_t[u2][:, :], score_bank[0][:, 0:P], ACT.Copy).then_inc(xs_t_ready, 1)

            def gelu(j, u2):
                act.wait_ge(hid_made, j + 1)
                nc.scalar.activation(hid[u2][:, :], score_bank[2 + u2][:, 0:F], ACT.Gelu).then_inc(hid_ready, 1)

            keep_rows_t(0, 0)

            def ffn(j, u4, turn, first, last):
                u2 = u4 % 2
                gelu(j, u2)
                if not last:
                    keep_rows_t(j + 1, 1 - u2)

            tiles(act, ffn)

        @block.gpsimd
        def _(pool):
            pool.memset(blank_row[:, 0:ROW - 1], 0.0).then_inc(blank_made, 1)
            pool.memset(blank_row[:, ROW - 1:ROW], float(2 * T)).then_inc(blank_made, 1)
            pool.memset(neg_half[:, :], -0.5).then_inc(blank_made, 1)
            pool.memset(eps[:, :], EPS).then_inc(blank_made, 1)
            pool.wait_ge(blank_made, 4)
            with pool.Fori(0, NT) as i:
                pool.dma_start(sorted_rows[bass.ts(i, P), :], blank_row[:, :]).then_inc(blanks_out, 16)

            def rstd(mv, ve, r, have, mid, done, n):
                pool.wait_ge(have, n)
                pool.tensor_tensor(ve[:, :], mv[:, 1:2], eps[:, :], ALU.add).then_inc(mid, 1)
                pool.wait_ge(mid, n)
                pool.tensor_tensor(r[:, :], ve[:, :], neg_half[:, :], ALU.pow).then_inc(done, 1)

            def add_bias(b, u, loads):
                pool.wait_ge(back_in[u], loads * 48)
                pool.tensor_tensor(x_plus_bias[u][:, :], x_sb[u][:, :], out_bias[:, :], ALU.add).then_inc(xb_ready, 1)

            def keep_row(p):
                alone(pool)
                pool.wait_ge(x2_ready, p + 1)
                pool.tensor_copy(rows[:, p, 0:D], x2[:, :]).then_inc(row_kept, 1)

            pool.wait_ge(weights_in, N_WEIGHTS)
            pool.wait_ge(prep, 3)

            def step(b, u, half, first, last):
                p = b - 1
                if not first:
                    rstd(mv1, ve1, rstd1, mv1_ready, ve1_ready, rstd1_ready, p + 1)
                add_bias(b, u, half(0) + 1)
                if not first:
                    rstd(mv2, ve2, rstd2, mv2_ready, ve2_ready, rstd2_ready, p + 1)
                    keep_row(p)

            batches(pool, step)
            p = B - 1
            rstd(mv1, ve1, rstd1, mv1_ready, ve1_ready, rstd1_ready, p + 1)
            rstd(mv2, ve2, rstd2, mv2_ready, ve2_ready, rstd2_ready, p + 1)
            keep_row(p)

            pool.wait_ge(blanks_out, 16 * NT)
            last_slot = pool.to_reg(NT * P - 1)
            with pool.Fori(2, 2 * (B // RS) + 2, 2) as both:
                for r in range(RS):
                    alone(pool)
                    pool.wait_ge(staged[r], both)
                    pool.indirect_dma_start(out=sorted_rows[:, :],
                                            out_offset=bass.IndirectOffsetOnAxis(ap=pos_stage[r][:, 0:1], axis=0),
                                            in_=row_stage[r][:, :], in_offset=None, bounds_check=last_slot,
                                            oob_is_err=False).then_inc(scattered[r], 16)

            last_token = pool.to_reg(T - 1)

            def finish(j, u4):
                rstd(mv3, ve3, rstd3, mv3_ready, ve3_ready, rstd3_ready, j + 1)
                alone(pool)
                pool.wait_ge(y2_ready, j + 1)
                pool.wait_ge(tok_ready, j + 1)
                pool.indirect_dma_start(out=out, out_offset=bass.IndirectOffsetOnAxis(ap=tok_i[u4][:, 0:1], axis=0),
                                        in_=y2[u4][:, :], in_offset=None, bounds_check=last_token,
                                        oob_is_err=False).then_inc(out_stored[u4], 16)

            with pool.Fori(0, NT // RS) as i:
                for u in range(RS):
                    finish(i * RS + u, u)
            for u in range(RS):
                pool.wait_ge(out_stored[u], 16 * (NT // RS))


def constants():
    c = np.zeros((P, C_N), np.float32)
    p = np.arange(P)
    row = p % 32
    c[:, C_ID:C_ID + P] = np.eye(P)
    c[:, C_TQ:C_TQ + P] = np.where((row == POS_ROW)[:, None], -p[None, :], 1)
    c[:, C_TK:C_TK + P] = np.where((row == SLOPE_ROW)[:, None], p[None, :], 1)
    c[:, C_KONE] = (row == SLOPE_ROW) | (row == POS_ROW) | (row == MAX_ROW)
    same = p[:, None] % E == p[None, :] % E
    c[:, C_SAME:C_SAME + P] = same
    c[:, C_BELOW:C_BELOW + P] = same & (p[:, None] < p[None, :])
    c[:, C_TRI:C_TRI + P] = p[:, None] < p[None, :]
    c[:, C_DESC:C_DESC + E] = E - np.arange(E)
    c[:, C_TILE:C_TILE + NT] = np.arange(NT)
    c[:, C_ONES:C_ONES + P] = 1
    c[:, C_TOK:C_TOK + T // P] = p[:, None] + P * np.arange(T // P)[None, :]
    return c


def by_group(rows):
    w = rows.reshape(NG, NC_, HD, *rows.shape[1:])
    out = np.zeros((NG, 32, NC_, *rows.shape[1:]), rows.dtype)
    out[:, :HD] = np.moveaxis(w, 1, 2)
    return out.reshape(P, NC_, *rows.shape[1:])


def kernel(**inputs):
    import concourse.bacc as bacc
    from concourse.bass_utils import run_bass_kernel_spmd

    a = {k: np.asarray(v) for k, v in inputs.items()}
    x, ctx = a["x"], a["ctx_1024"]
    slopes = np.zeros((NG, 32, NC_), np.float32)
    slopes[:, SLOPE_ROW] = slopes[:, POS_ROW] = a["L0_attn_slopes"].reshape(NG, NC_)
    wo_t = np.zeros((NG, NC_, HD, NC_, D), np.float32)
    for c in range(NC_):
        wo_t[:, c, :, c] = a["L0_attn_Wo"].T.reshape(NG, NC_, HD, D)[:, c]
    arrays = {
        "x": x, "xt": x.transpose(0, 2, 1), "ctx": ctx, "ctxt": ctx.transpose(0, 2, 1),
        "wq": by_group(a["L0_attn_Wq"]).transpose(2, 1, 0), "wk": by_group(a["L0_attn_Wk"]).transpose(2, 1, 0),
        "wv": a["L0_attn_Wv"].T, "wo": wo_t.reshape(P, NC_, D),
        "bq": by_group(a["L0_attn_bq"]), "bk": by_group(a["L0_attn_bk"]), "slopes": slopes.reshape(P, NC_),
        "bv": a["L0_attn_bv"].reshape(P, 1), "bo": a["L0_attn_bo"].reshape(1, P),
        "wg": a["L0_ffn_Wg"], "w1": a["L0_ffn_W1"], "w2": a["L0_ffn_W2"], "consts": constants(),
    }
    nc = bacc.Bacc("TRN2", target_bir_lowering=False, num_devices=1)
    arrays = {f"in_{k}": np.ascontiguousarray(v) for k, v in arrays.items()}
    args = [nc.dram_tensor(k, v.shape, mybir.dt.from_np(v.dtype), kind="ExternalInput").ap() for k, v in arrays.items()]
    result = nc.dram_tensor("result", (T, D), F32, kind="ExternalOutput").ap()
    attention_ffn(nc, *args, result)
    r = run_bass_kernel_spmd(nc, [arrays], core_ids=[0])
    return r.results[0]["result"].reshape(B, S, D)
```

```python
from contextlib import ExitStack

import numpy as np

import concourse.bass as bass
from concourse import mybir

ACT = mybir.ActivationFunctionType
ALU = mybir.AluOpType
AX = mybir.AxisListType
F32 = mybir.dt.float32
BF16 = mybir.dt.bfloat16
I32 = mybir.dt.int32
F32R = mybir.dt.float32r

P = 128
B, S, D = 64, 128, 128
SK = 120
H, HD = 16, 8
NG, NC_ = 4, 4
E, F = 8, 256
T = B * S
CAP = max(1, T // E)
NT = T // P + E
ROW = D + 2
EPS = 1e-5
PROB_BITS = 30
SLOPE_ROW, POS_ROW, MAX_ROW = 3 * HD, 3 * HD + 2, 3 * HD + 4
VW = 5 * HD

C_ID, C_TQ, C_KAUG, C_SAME, C_BELOW, C_TRI = (i * P for i in range(6))
C_QH, C_QL, C_KH, C_KL = (6 * P + i * NC_ * P for i in range(4))
C_V, C_D = (6 * P + 4 * NC_ * P + i * 2 * P for i in range(2))
C_DESC = C_D + 2 * P
C_TILE = C_DESC + E
C_ONES = C_TILE + NT
C_LOW = C_ONES + P
C_TOK = C_LOW + 1
C_N = C_TOK + T // P


def attention_ffn(nc, x, xt, ctx_in, ctxt, wq, wk, wv, wo, bq, bk, slopes, bv, bo, wg, w1, w2, consts, out):
    st = ExitStack()
    with st:
        def sb(name, shape, dt=F32):
            return st.enter_context(nc.sbuf_tensor(name, shape, dt))

        def bank(name):
            return st.enter_context(nc.psum_tensor(name, [P, 512], F32))

        def sem(name):
            return st.enter_context(nc.semaphore(name))

        sorted_rows = nc.dram_tensor("sorted_rows", [NT * P, ROW], F32, kind="Internal").ap()

        cst = sb("cst", [P, C_N])
        ident = cst[:, C_ID:C_ID + P]
        wq_sb, wk_sb, wv_sb, wo_sb = (sb(n, [P, P]) for n in ("wq_sb", "wk_sb", "wv_sb", "wo_sb"))
        wg_sb = sb("wg_sb", [P, E])
        w1_sb, w2_sb = sb("w1_sb", [P, E, F]), sb("w2_sb", [P, E, 2, D])
        bq_sb, bk_sb, sl_sb = sb("bq_sb", [P, 1]), sb("bk_sb", [P, 1]), sb("sl_sb", [P, NC_])
        bv_sb, bo_sb = sb("bv_sb", [P, 1]), sb("bo_sb", [1, P])
        ident_r = sb("ident_r", [P, P], F32R)
        spread = {n: sb(f"spread_{n}", [P, NC_, P], F32R) for n in ("qh", "ql", "kh", "kl")}
        q_rows_added, k_rows_added = sb("q_rows_added", [P, NC_, P], F32R), sb("k_rows_added", [P, NC_, P], F32R)
        aug, aug_h = sb("aug", [P, NC_, P]), sb("aug_h", [P, NC_, P], F32R)
        bv_wide, out_bias = sb("bv_wide", [P, P]), sb("out_bias", [P, P])
        tri_bf, ones_bf = sb("tri_bf", [P, P], BF16), sb("ones_bf", [P, P], BF16)
        neg_half, eps = sb("neg_half", [P, 1]), sb("eps", [P, 1])
        blank_row = sb("blank_row", [P, ROW])

        xt_sb = [sb(f"xt_sb{u}", [P, P]) for u in range(2)]
        x_sb = [sb(f"x_sb{u}", [P, P]) for u in range(2)]
        c_sb = [sb(f"c_sb{u}", [SK, P]) for u in range(2)]
        ct_sb = [sb(f"ct_sb{u}", [P, SK]) for u in range(2)]
        x_plus_bias = [sb(f"x_plus_bias{u}", [P, P]) for u in range(2)]
        q_hi, q_lo, k_hi, k_lo = (sb(n, [P, P], F32R) for n in ("q_hi", "q_lo", "k_hi", "k_lo"))
        qt = [sb(f"qt{u}", [P, NC_, P], F32R) for u in range(2)]
        kt = [sb(f"kt{u}", [P, NC_, P], F32R) for u in range(2)]
        v_sb = [sb(f"v_sb{u}", [P, H, VW]) for u in range(2)]
        q_less_max = sb("q_less_max", [P, NC_, P], F32R)
        neg_max = sb("neg_max", [P, NG, NC_])
        max_rows = sb("max_rows", [P, NC_, P], F32R)
        probs_t = sb("probs_t", [P, NG, 512])
        sums = sb("sums", [P, 2, P])
        den_rec, heads_out = sb("den_rec", [P, P]), sb("heads_out", [P, P])
        t1, x1, t2, x2 = (sb(n, [P, P]) for n in ("t1", "x1", "t2", "x2"))
        x1t, x2t, p2, p2t = sb("x1t", [P, P]), sb("x2t", [P, P]), sb("p2", [P, SK]), sb("p2t", [SK, P])
        stats1, stats2 = sb("stats1", [P, 6]), sb("stats2", [P, 6])
        mv1, mv2 = sb("mv1", [P, 2]), sb("mv2", [P, 2])
        ve1, ve2, rstd1, rstd2 = (sb(n, [P, 1]) for n in ("ve1", "ve2", "rstd1", "rstd2"))
        neg_max2, sum2, rec2 = (sb(n, [P, 1]) for n in ("neg_max2", "sum2", "rec2"))
        rows = sb("rows", [P, B, ROW])

        proj_bank, query_bank, value_bank, tail_bank = (
            bank(n) for n in ("proj_bank", "query_bank", "value_bank", "tail_bank"))
        score_bank = [bank(f"score_bank{g}") for g in range(NG)]
        slot = [tail_bank[:, i * P:(i + 1) * P] for i in range(4)]

        logits = sb("logits", [P, B, E])
        tok_a, tok_b, tok_c, prob = (sb(n, [P, B, E]) for n in ("tok_a", "tok_b", "tok_c", "prob"))
        ro_t, ro_u, weight = sb("ro_t", [P, B]), sb("ro_u", [P, B]), sb("weight", [P, B])
        prob_e, ex_a, ex_b, ex_c = (sb(n, [P, 512]) for n in ("prob_e", "ex_a", "ex_b", "ex_c"))
        thr, cand, keep, cnt, cnt2 = (sb(n, [P, 1]) for n in ("thr", "cand", "keep", "cnt", "cnt2"))
        bit = sb("bit", [P, 1], I32)
        need, before = sb("need", [P, 1]), sb("before", [P, 1])
        onehot_bf = sb("onehot_bf", [P, E, B], BF16)
        e_f = [sb(f"e_f{i}", [P, E]) for i in range(5)]
        e_i, e_i2 = sb("e_i", [P, E], I32), sb("e_i2", [P, E], I32)
        tile_cmp = sb("tile_cmp", [P, NT, E - 1])
        tile_e, tile_ei = sb("tile_e", [P, NT]), sb("tile_ei", [P, NT], I32)
        pos_f = sb("pos_f", [P, B])

        RS = 4
        row_stage = [sb(f"row_stage{i}", [P, ROW]) for i in range(RS)]
        pos_stage = [sb(f"pos_stage{i}", [P, 1], I32) for i in range(RS)]
        xs = [sb(f"xs{i}", [P, ROW]) for i in range(RS)]
        xs_t = [sb(f"xs_t{i}", [P, P]) for i in range(2)]
        hid = [sb(f"hid{i}", [P, F]) for i in range(2)]
        hid_t = sb("hid_t", [P, 2, P])
        y1 = sb("y1", [P, P])
        y2 = [sb(f"y2_{i}", [P, P]) for i in range(RS)]
        tok_i = [sb(f"tok_i{i}", [P, 1], I32) for i in range(RS)]
        stats3, mv3, ve3, rstd3 = sb("stats3", [P, 6]), sb("mv3", [P, 2]), sb("ve3", [P, 1]), sb("rstd3", [P, 1])

        names = """weights_in prep blank_made front_in0 front_in1 back_in0 back_in1 blanks_out
        qkv_made k_spread q_spread scored max_added rescored summed compacted projected x1_turned scored2 p2_turned
        attended2 x2_turned gated bias_made
        hi_ready lo_ready k_ready q_ready max_ready max_hi_ready max_lo_ready qm_ready sums_ready den_ready heads_ready t1_ready st1_ready mv1_ready x1_ready
        max2_ready rec2_ready t2_ready st2_ready mv2_ready x2_ready logits_ready
        x1t_ready p2_ready v_ready p2t_ready probs_ready x2t_ready
        xb_ready ve1_ready rstd1_ready ve2_ready rstd2_ready row_kept
        dve_step gate_max_ready gate_exp gates_turned counted sel_turned ranked found searched bit_ready
        table_ready staged0 staged1 staged2 staged3 scattered0 scattered1 scattered2 scattered3 xs_in0 xs_in1 xs_in2 xs_in3
        xs_turned xs_t_ready hid_made hid_ready hid_turned hid_t_ready y_made y1_ready st3_ready mv3_ready ve3_ready
        rstd3_ready y2_ready tok_ready out_stored0 out_stored1 out_stored2 out_stored3""".split()
        s = {n: sem(n) for n in names}
        (weights_in, prep, blank_made, front_in0, front_in1, back_in0, back_in1, blanks_out,
         qkv_made, k_spread, q_spread, scored, max_added, rescored, summed, compacted, projected, x1_turned, scored2,
         p2_turned,
         attended2, x2_turned, gated, bias_made,
         hi_ready, lo_ready, k_ready, q_ready, max_ready, max_hi_ready, max_lo_ready, qm_ready, sums_ready, den_ready, heads_ready, t1_ready, st1_ready, mv1_ready, x1_ready,
         max2_ready, rec2_ready, t2_ready, st2_ready, mv2_ready, x2_ready, logits_ready,
         x1t_ready, p2_ready, v_ready, p2t_ready, probs_ready, x2t_ready,
         xb_ready, ve1_ready, rstd1_ready, ve2_ready, rstd2_ready, row_kept,
         dve_step, gate_max_ready, gate_exp, gates_turned, counted, sel_turned, ranked, found, searched, bit_ready,
         table_ready, staged0, staged1, staged2, staged3, scattered0, scattered1, scattered2, scattered3,
         xs_in0, xs_in1, xs_in2, xs_in3,
         xs_turned, xs_t_ready, hid_made, hid_ready, hid_turned, hid_t_ready, y_made, y1_ready, st3_ready, mv3_ready,
         ve3_ready, rstd3_ready, y2_ready, tok_ready, out_stored0, out_stored1, out_stored2,
         out_stored3) = (s[n] for n in names)
        front_in, back_in = [front_in0, front_in1], [back_in0, back_in1]
        staged = [staged0, staged1, staged2, staged3]
        scattered = [scattered0, scattered1, scattered2, scattered3]
        xs_in = [xs_in0, xs_in1, xs_in2, xs_in3]
        out_stored = [out_stored0, out_stored1, out_stored2, out_stored3]
        N_WEIGHTS = 15 * 16

        def ge(eng, semaphore, value):
            if not (isinstance(value, int) and value <= 0):
                eng.wait_ge(semaphore, value)

        def alone(eng):
            eng.wait_ge(weights_in, N_WEIGHTS)

        def batches(eng, step):
            def peeled(b):
                step(b, b % 2, lambda d: (b + d) // 2, (b + 1 < B, b < B, 1 <= b <= B, b >= 2))

            for b in range(3):
                peeled(b)
            with eng.Fori(0, (B - 4) // 2) as i:
                for u in range(2):
                    step(i * 2 + (3 + u), (3 + u) % 2, lambda d: i + (3 + u + d) // 2, (True,) * 4)
            for b in range(B - 1, B + 2):
                peeled(b)

        def tiles(eng, step):
            lead = RS + 1
            for j in range(lead):
                step(j, j % RS, lambda d: (j + d) // RS, j == 0, False)
            n = (NT - 1 - lead) // RS
            with eng.Fori(0, n) as i:
                for u in range(RS):
                    step(i * RS + (lead + u), (lead + u) % RS, lambda d: i + (lead + u + d) // RS, False, False)
            for j in range(lead + n * RS, NT):
                step(j, j % RS, lambda d: (j + d) // RS, False, j == NT - 1)

        block = st.enter_context(nc.Block())

        @block.sync
        def _(sp):
            def front(n, u):
                sp.dma_start(xt_sb[u][:, :], xt[n]).then_inc(front_in[u], 16)

            def back(n, u):
                sp.dma_start(x_sb[u][:, :], x[n]).then_inc(back_in[u], 16)
                sp.dma_start(c_sb[u][:, :], ctx_in[n]).then_inc(back_in[u], 16)
                sp.dma_start(ct_sb[u][:, :], ctxt[n]).then_inc(back_in[u], 16)

            front(0, 0)
            back(0, 0)
            front(1, 1)
            back(1, 1)
            sp.wait_ge(qkv_made, 1)
            front(2, 0)
            sp.wait_ge(qkv_made, 2)
            front(3, 1)

            def turn(b, u):
                sp.wait_ge(attended2, b - 1)
                sp.wait_ge(xb_ready, b - 1)
                back(b, u)
                if not isinstance(b, int) or b + 2 < B:
                    sp.wait_ge(qkv_made, b + 1)
                    front(b + 2, u)

            with sp.Fori(0, (B - 4) // 2) as i:
                for v in range(2):
                    turn(i * 2 + (2 + v), v)
            turn(B - 2, 0)
            turn(B - 1, 1)

            for r in range(RS):
                sp.wait_ge(scattered[r], 16 * (B // RS))

            def load_rows(j, u):
                sp.dma_start(xs[u][:, :], sorted_rows[bass.ts(j, P), :]).then_inc(xs_in[u], 16)

            for j in range(RS):
                load_rows(j, j)
            with sp.Fori(0, NT // RS - 1) as i:
                for u in range(RS):
                    j = i * RS + u
                    sp.wait_ge(y1_ready, j + 1)
                    sp.wait_ge(tok_ready, j + 1)
                    load_rows(j + RS, u)

        @block.tensor
        def _(pe):
            def project(n, u, loads):
                pe.wait_ge(front_in[u], loads * 16)
                ge(pe, k_ready, n)
                pe.matmul(proj_bank[:, 0:P], wk_sb[:, :], xt_sb[u][:, :], start=True, stop=True)
                pe.matmul(proj_bank[:, P:2 * P], wq_sb[:, :], xt_sb[u][:, :], start=True, stop=True)
                pe.matmul(proj_bank[:, 2 * P:3 * P], xt_sb[u][:, :], wv_sb[:, :], start=True,
                          stop=True).then_inc(qkv_made, 1)

            def spread_rows(dst, added, hi, lo, to_hi, to_lo):
                for c in range(NC_):
                    pe.matmul(dst[:, c * P:(c + 1) * P], to_hi[:, c, :], hi[:, :], start=(c == 0), stop=False,
                              skip_group_check=True)
                    pe.matmul(dst[:, c * P:(c + 1) * P], to_lo[:, c, :], lo[:, :], start=False, stop=False,
                              skip_group_check=True)
                return pe.matmul(dst[:, :], ident_r[:, :], added[:, :, :], start=False, stop=True,
                                 skip_group_check=True)

            def spread_keys(n):
                pe.wait_ge(lo_ready, n + 1)
                spread_rows(proj_bank, k_rows_added, k_hi, k_lo, spread["kh"], spread["kl"]).then_inc(k_spread, 1)

            def spread_queries(n):
                pe.wait_ge(lo_ready, n + 1)
                ge(pe, qm_ready, n)
                spread_rows(query_bank, q_rows_added, q_hi, q_lo, spread["qh"], spread["ql"]).then_inc(q_spread, 1)

            def score(b, u, g):
                if g == 0:
                    pe.wait_ge(k_ready, b + 1)
                    pe.wait_ge(q_ready, b + 1)
                ge(pe, probs_ready, 4 * b + g - 3)
                r = slice(32 * g, 32 * g + 32)
                for c in range(NC_):
                    mm = pe.matmul(score_bank[g][:, c * P:(c + 1) * P], qt[u][r, c, :], kt[u][r, c, :],
                                   start=True, stop=True, tile_position=(32 * g, 0))
                mm.then_inc(scored, 1)

            def add_max(b):
                pe.wait_ge(max_lo_ready, b + 1)
                for c in range(NC_):
                    mm = pe.matmul(query_bank[:, c * P:(c + 1) * P], max_rows[:, c, :], ident_r[:, :], start=False,
                                   stop=True, skip_group_check=True)
                mm.then_inc(max_added, 1)

            def rescore(b, u, g):
                if g == 0:
                    pe.wait_ge(qm_ready, b + 1)
                r = slice(32 * g, 32 * g + 32)
                for c in range(NC_):
                    mm = pe.matmul(score_bank[g][:, c * P:(c + 1) * P], kt[u][r, c, :], q_less_max[r, c, :],
                                   start=True, stop=True, tile_position=(32 * g, 0))
                mm.then_inc(rescored, 1)

            def sum_values(p, u):
                pe.wait_ge(probs_ready, 4 * p + 4)
                for c in range(NC_):
                    w = slice(HD, VW) if c % 2 == 0 else slice(0, VW - HD)
                    q = slice((c // 2) * P, (c // 2 + 1) * P)
                    for g in range(NG):
                        r = slice(32 * g, 32 * g + 32)
                        mm = pe.matmul(value_bank[r, q], v_sb[u][:, NC_ * g + c, w],
                                       probs_t[:, g, c * P:(c + 1) * P], start=(c % 2 == 0), stop=(c % 2 == 1),
                                       tile_position=(0, 32 * g))
                mm.then_inc(summed, 1)

            def compact(p):
                pe.wait_ge(sums_ready, p + 1)
                for i, base in enumerate((C_V, C_D)):
                    for t in range(2):
                        mm = pe.matmul(value_bank[:, (2 + i) * P:(3 + i) * P], cst[:, base + t * P:base + (t + 1) * P],
                                       sums[:, t, :], start=(t == 0), stop=(t == 1))
                mm.then_inc(compacted, 1)

            def project_out(p):
                pe.wait_ge(heads_ready, p + 1)
                ge(pe, logits_ready, p)
                pe.matmul(slot[0], heads_out[:, :], wo_sb[:, :], start=True, stop=True).then_inc(projected, 1)

            def turn_x1(p):
                pe.wait_ge(x1_ready, p + 1)
                pe.transpose(slot[1], x1[:, :], ident).then_inc(x1_turned, 1)

            def score2(p, u, loads):
                pe.wait_ge(back_in[u], loads * 48)
                pe.wait_ge(x1t_ready, p + 1)
                pe.matmul(slot[2][:, 0:SK], x1t[:, :], ct_sb[u][:, :], start=True, stop=True).then_inc(scored2, 1)

            def turn_p2(p):
                pe.wait_ge(p2_ready, p + 1)
                pe.transpose(slot[3][0:SK, :], p2[:, :], ident).then_inc(p2_turned, 1)

            def attend2(p, u):
                pe.wait_ge(p2t_ready, p + 1)
                pe.wait_ge(t1_ready, p + 1)
                pe.matmul(slot[0], p2t[:, :], c_sb[u][:, :], start=True, stop=True).then_inc(attended2, 1)

            def turn_x2(p):
                pe.wait_ge(x2_ready, p + 1)
                pe.transpose(slot[1], x2[:, :], ident).then_inc(x2_turned, 1)

            def gate(p):
                pe.wait_ge(x2t_ready, p + 1)
                pe.wait_ge(p2_ready, p + 1)
                pe.matmul(slot[2][:, 0:E], x2t[:, :], wg_sb[:, :], start=True, stop=True).then_inc(gated, 1)

            pe.wait_ge(weights_in, N_WEIGHTS)
            pe.wait_ge(prep, 1)
            pe.matmul(slot[0], bv_wide[:, :], wo_sb[:, :], start=True, stop=False)
            pe.matmul(slot[0], cst[0:1, C_ONES:C_ONES + P], bo_sb[:, :], start=False, stop=True).then_inc(bias_made, 1)
            pe.wait_ge(prep, 2)
            project(0, 0, 1)
            spread_keys(0)
            spread_queries(0)

            def step(b, u, half, stages):
                proj, sco, val, tail = stages
                n, p, t, w = b + 1, b - 1, b - 2, 1 - u
                if tail:
                    project_out(t)
                if sco:
                    for g in range(NG):
                        score(b, u, g)
                if val:
                    sum_values(p, w)
                if tail:
                    turn_x1(t)
                    score2(t, u, half(-2) + 1)
                if proj:
                    project(n, w, half(1) + 1)
                if sco:
                    add_max(b)
                if val:
                    compact(p)
                if tail:
                    turn_p2(t)
                if proj:
                    spread_keys(n)
                if sco:
                    rescore(b, u, 0)
                    rescore(b, u, 1)
                if tail:
                    attend2(t, u)
                if sco:
                    rescore(b, u, 2)
                    rescore(b, u, 3)
                if proj:
                    spread_queries(n)
                if tail:
                    turn_x2(t)
                    gate(t)

            batches(pe, step)

            pe.wait_ge(found, 1)
            for b4 in range(4):
                mm = pe.transpose(score_bank[0][:, b4 * P:(b4 + 1) * P], ex_b[:, b4 * P:(b4 + 1) * P], ident)
            mm.then_inc(gates_turned, 1)

            def count(n, rhs, weights, dst):
                pe.wait_ge(searched, n)
                pe.matmul(dst, weights, rhs, start=True, stop=True).then_inc(counted, 1)

            same = cst[:, C_SAME:C_SAME + P]
            with pe.Fori(0, PROB_BITS) as i:
                count(i + 1, cnt[:, :], same, score_bank[1][:, 0:1])
            count(PROB_BITS + 1, cnt[:, :], same, score_bank[1][:, 0:1])
            count(PROB_BITS + 2, cnt2[:, :], cst[:, C_BELOW:C_BELOW + P], score_bank[1][:, 1:2])
            pe.wait_ge(found, 2)
            for b4 in range(4):
                mm = pe.transpose(score_bank[0][:, b4 * P:(b4 + 1) * P], ex_a[:, b4 * P:(b4 + 1) * P], ident)
            mm.then_inc(sel_turned, 1)
            pe.wait_ge(found, 3)
            pe.matmul(score_bank[1][:, :], tri_bf[:, :], onehot_bf[:, :, :], start=True, stop=True)
            pe.matmul(score_bank[2][:, :], ones_bf[:, :], onehot_bf[:, :, :], start=True, stop=True).then_inc(ranked, 1)

            y_bank = [tail_bank, proj_bank]
            h_bank = [score_bank[2], score_bank[3]]

            def turn_rows(j, u4, loads):
                pe.wait_ge(xs_in[u4], loads * 16)
                pe.transpose(score_bank[0][:, 0:P], xs[u4][:, 0:D], ident).then_inc(xs_turned, 1)

            def hidden(j, u2):
                e = pe.value_load(tile_ei[0:1, bass.ds(j, 1)], min_val=0, max_val=E - 1)
                pe.wait_ge(xs_t_ready, j + 1)
                pe.matmul(h_bank[u2][:, 0:F], xs_t[u2][:, :], w1_sb[:, e, :], start=True, stop=True).then_inc(hid_made, 1)

            def turn_hidden(j, u2):
                pe.wait_ge(hid_ready, j + 1)
                pe.transpose(value_bank[:, 0:P], hid[u2][:, 0:P], ident)
                pe.transpose(value_bank[:, P:2 * P], hid[u2][:, P:2 * P], ident).then_inc(hid_turned, 1)

            def back_to_rows(j, u2):
                e = pe.value_load(tile_ei[0:1, bass.ds(j, 1)], min_val=0, max_val=E - 1)
                pe.wait_ge(hid_t_ready, j + 1)
                pe.matmul(y_bank[u2][:, 0:D], hid_t[:, 0, :], w2_sb[:, e, 0, :], start=True, stop=False)
                pe.matmul(y_bank[u2][:, 0:D], hid_t[:, 1, :], w2_sb[:, e, 1, :], start=False, stop=True).then_inc(y_made, 1)

            pe.wait_ge(table_ready, 1)
            turn_rows(0, 0, 1)

            def ffn(j, u4, turn, first, last):
                u2 = u4 % 2
                hidden(j, u2)
                if not first:
                    turn_hidden(j - 1, 1 - u2)
                if not last:
                    turn_rows(j + 1, (u4 + 1) % RS, turn(1) + 1)
                if not first:
                    back_to_rows(j - 1, 1 - u2)

            tiles(pe, ffn)
            turn_hidden(NT - 1, (NT - 1) % 2)
            back_to_rows(NT - 1, (NT - 1) % 2)

        @block.vector
        def _(dve):
            steps = [0]

            def then(ins):
                steps[0] += 1
                ins.then_inc(dve_step, 1)
                dve.wait_ge(dve_step, steps[0])

            for u in range(2):
                then(dve.memset(v_sb[u][:, :, :], 0.0))
                then(dve.memset(v_sb[u][:, :, 3 * HD:4 * HD], 1.0))
            then(dve.memset(max_rows[:, :, :].bitcast(F32), 0.0))
            dve.wait_ge(weights_in, N_WEIGHTS)
            then(dve.memset(bv_wide[:, :], 0.0))
            dve.tensor_scalar(bv_wide[:, :], bv_wide[:, :], bv_sb[:, 0:1], None, ALU.add).then_inc(prep, 1)
            then(dve.tensor_scalar(bq_sb[:, :], bq_sb[:, :], HD ** -0.5, None, ALU.mult))
            then(dve.tensor_copy(ident_r[:, :], ident))
            for name, at in (("qh", C_QH), ("ql", C_QL), ("kh", C_KH), ("kl", C_KL)):
                then(dve.tensor_copy(spread[name][:, :, :],
                                     cst[:, at:at + NC_ * P].rearrange("p (c r) -> p c r", c=NC_)))
            for c in range(NC_):
                then(dve.tensor_copy(k_rows_added[:, c, :], cst[:, C_KAUG:C_KAUG + P]))
                then(dve.tensor_scalar(aug[:, c, :], cst[:, C_TQ:C_TQ + P], sl_sb[:, c:c + 1], None, ALU.mult))
            then(dve.tensor_scalar(aug_h[:, :, :], aug[:, :, :], cst[:, C_LOW:C_LOW + 1], None, ALU.mult))
            then(dve.tensor_tensor(q_rows_added[:, :, :], aug[:, :, :], aug_h[:, :, :].bitcast(F32), ALU.subtract))
            then(dve.tensor_copy(tri_bf[:, :], cst[:, C_TRI:C_TRI + P]))
            then(dve.memset(ones_bf[:, :], 1.0))
            dve.tensor_scalar(wq_sb[:, :], wq_sb[:, :], HD ** -0.5, None, ALU.mult).then_inc(prep, 1)
            dve.wait_ge(bias_made, 1)
            dve.tensor_copy(out_bias[:, :], slot[0]).then_inc(prep, 1)

            def low_parts(n):
                dve.wait_ge(hi_ready, n + 1)
                dve.scalar_tensor_tensor(k_lo[:, :], proj_bank[:, 0:P], bk_sb[:, 0:1], k_hi[:, :].bitcast(F32),
                                         ALU.add, ALU.subtract)
                dve.scalar_tensor_tensor(q_lo[:, :], proj_bank[:, P:2 * P], bq_sb[:, 0:1], q_hi[:, :].bitcast(F32),
                                         ALU.add, ALU.subtract).then_inc(lo_ready, 1)

            def row_max(b, g):
                dve.wait_ge(scored, 4 * b + g + 1)
                dve.tensor_reduce(neg_max[:, g, :], score_bank[g][:, :].rearrange("p (c k) -> p c k", c=NC_),
                                  AX.X, ALU.max, negate=True).then_inc(max_ready, 1)

            max_view = max_rows[:, :, :].rearrange("p c (g r) -> p g c r", g=NG)

            def split_max(b):
                dve.wait_ge(max_ready, 4 * b + 4)
                ge(dve, max_added, b)
                dve.tensor_copy(max_view[:, :, :, MAX_ROW], neg_max[:, :, :]).then_inc(max_hi_ready, 1)
                dve.wait_ge(max_hi_ready, b + 1)
                dve.tensor_tensor(max_view[:, :, :, MAX_ROW + 1], neg_max[:, :, :],
                                  max_view[:, :, :, MAX_ROW].bitcast(F32), ALU.subtract).then_inc(max_lo_ready, 1)

            def normalise(p):
                dve.wait_ge(compacted, p + 1)
                dve.reciprocal(den_rec[:, :], value_bank[:, 3 * P:4 * P]).then_inc(den_ready, 1)
                dve.wait_ge(den_ready, p + 1)
                dve.tensor_tensor(heads_out[:, :], value_bank[:, 2 * P:3 * P], den_rec[:, :],
                                  ALU.mult).then_inc(heads_ready, 1)

            def residual1(p, u):
                dve.wait_ge(projected, p + 1)
                dve.wait_ge(xb_ready, p + 1)
                dve.tensor_tensor(t1[:, :], slot[0], x_plus_bias[u][:, :], ALU.add).then_inc(t1_ready, 1)
                dve.wait_ge(t1_ready, p + 1)
                dve.bn_stats(stats1[:, :], t1[:, :]).then_inc(st1_ready, 1)
                alone(dve)
                dve.wait_ge(st1_ready, p + 1)
                dve.bn_aggr(mv1[:, :], stats1[:, :]).then_inc(mv1_ready, 1)

            def norm1(p):
                dve.wait_ge(rstd1_ready, p + 1)
                dve.tensor_scalar(x1[:, :], t1[:, :], mv1[:, 0:1], rstd1[:, 0:1], ALU.subtract,
                                  ALU.mult).then_inc(x1_ready, 1)

            def row_max2(p):
                dve.wait_ge(scored2, p + 1)
                dve.tensor_reduce(neg_max2[:, :], slot[2][:, 0:SK], AX.X, ALU.max, negate=True).then_inc(max2_ready, 1)

            def residual2(p):
                dve.wait_ge(p2_ready, p + 1)
                dve.reciprocal(rec2[:, :], sum2[:, :]).then_inc(rec2_ready, 1)
                dve.wait_ge(rec2_ready, p + 1)
                dve.wait_ge(attended2, p + 1)
                dve.scalar_tensor_tensor(t2[:, :], slot[0], rec2[:, 0:1], x1[:, :], ALU.mult,
                                         ALU.add).then_inc(t2_ready, 1)
                dve.wait_ge(t2_ready, p + 1)
                dve.bn_stats(stats2[:, :], t2[:, :]).then_inc(st2_ready, 1)
                alone(dve)
                dve.wait_ge(st2_ready, p + 1)
                dve.bn_aggr(mv2[:, :], stats2[:, :]).then_inc(mv2_ready, 1)

            def norm2(p):
                dve.wait_ge(rstd2_ready, p + 1)
                dve.tensor_scalar(x2[:, :], t2[:, :], mv2[:, 0:1], rstd2[:, 0:1], ALU.subtract,
                                  ALU.mult).then_inc(x2_ready, 1)

            def keep_logits(p):
                dve.wait_ge(gated, p + 1)
                dve.tensor_copy(logits[:, p, :], slot[2][:, 0:E]).then_inc(logits_ready, 1)

            low_parts(0)

            def step(b, u, half, stages):
                proj, sco, val, tail = stages
                n, p, t = b + 1, b - 1, b - 2
                if tail:
                    residual1(t, u)
                if sco:
                    row_max(b, 0)
                    row_max(b, 1)
                if tail:
                    norm1(t)
                if sco:
                    row_max(b, 2)
                    row_max(b, 3)
                    split_max(b)
                if tail:
                    row_max2(t)
                if proj:
                    low_parts(n)
                if val:
                    normalise(p)
                if tail:
                    residual2(t)
                    norm2(t)
                    keep_logits(t)

            batches(dve, step)

            def over_e(a):
                return a.unsqueeze(2).broadcast_to([P, B, E])

            dve.wait_ge(logits_ready, B)
            then(dve.tensor_reduce(ro_t[:, :], logits[:, :, :], AX.X, ALU.max))
            dve.tensor_tensor(tok_a[:, :, :], logits[:, :, :], over_e(ro_t[:, :]), ALU.subtract).then_inc(gate_max_ready, 1)
            dve.wait_ge(gate_exp, 1)
            then(dve.tensor_reduce(ro_t[:, :], tok_b[:, :, :], AX.X, ALU.add))
            then(dve.reciprocal(ro_u[:, :], ro_t[:, :]))
            then(dve.tensor_tensor(prob[:, :, :], tok_b[:, :, :], over_e(ro_u[:, :]), ALU.mult))
            dve.tensor_copy(ex_b[:, :].rearrange("p (b i e) -> p b i e", b=4, e=E),
                            prob[:, :, :].rearrange("p (i b) e -> p b i e", b=4)).then_inc(found, 1)

            then(dve.memset(thr[:, :], 0.0))
            then(dve.memset(bit[:, :], 1 << (PROB_BITS - 1)))
            dve.wait_ge(gates_turned, 1)
            then(dve.tensor_copy(prob_e[:, :], score_bank[0][:, :]))
            base = steps[0]
            with dve.Fori(0, PROB_BITS) as i:
                dve.tensor_tensor(cand[:, :].bitcast(I32), thr[:, :].bitcast(I32), bit[:, :],
                                  ALU.bitwise_or).then_inc(dve_step, 1)
                dve.wait_ge(dve_step, i * 4 + (base + 1))
                dve.tensor_scalar(ex_a[:, :], prob_e[:, :], cand[:, 0:1], None, ALU.is_ge, ALU.add,
                                  accum_out=cnt[:, :]).then_inc(searched, 1)
                dve.tensor_scalar(bit[:, :], bit[:, :], 1, None, ALU.logical_shift_right).then_inc(dve_step, 1)
                dve.wait_ge(counted, i + 1)
                dve.tensor_scalar(keep[:, :], score_bank[1][:, 0:1], float(CAP), cand[:, 0:1], ALU.is_ge,
                                  ALU.mult).then_inc(dve_step, 1)
                dve.wait_ge(dve_step, i * 4 + (base + 3))
                dve.tensor_tensor(thr[:, :], thr[:, :], keep[:, :], ALU.max).then_inc(dve_step, 1)
                dve.wait_ge(dve_step, i * 4 + (base + 4))
            steps[0] += 4 * PROB_BITS

            dve.tensor_scalar(ex_a[:, :], prob_e[:, :], thr[:, 0:1], None, ALU.is_gt, ALU.add,
                              accum_out=cnt[:, :]).then_inc(searched, 1)
            dve.tensor_scalar(ex_b[:, :], prob_e[:, :], thr[:, 0:1], None, ALU.is_equal, ALU.add,
                              accum_out=cnt2[:, :]).then_inc(searched, 1)
            dve.wait_ge(searched, PROB_BITS + 2)
            then(dve.tensor_tensor_scan(ex_c[:, :], cst[:, C_ONES:C_ONES + 1].broadcast_to([P, 512]),
                                        ex_b[:, :], 0.0, ALU.mult, ALU.add))
            dve.wait_ge(counted, PROB_BITS + 2)
            then(dve.tensor_scalar(need[:, :], score_bank[1][:, 0:1], -1.0, float(CAP), ALU.mult, ALU.add))
            then(dve.tensor_copy(before[:, :], score_bank[1][:, 1:2]))
            then(dve.tensor_scalar(ex_c[:, :], ex_c[:, :], before[:, 0:1], need[:, 0:1], ALU.add, ALU.is_le))
            then(dve.tensor_tensor(ex_c[:, :], ex_c[:, :], ex_b[:, :], ALU.mult))
            dve.tensor_tensor(ex_a[:, :], ex_a[:, :], ex_c[:, :], ALU.add).then_inc(found, 1)

            dve.wait_ge(sel_turned, 1)
            sel = tok_a
            sv = sel[:, :, :].rearrange("p (i b) e -> p b i e", b=4)
            kb = score_bank[0][:, :].rearrange("p (b i e) -> p b i e", b=4, e=E)
            then(dve.tensor_copy(sv, kb))
            then(dve.tensor_tensor(tok_b[:, :, :], prob[:, :, :], sel[:, :, :], ALU.mult))
            then(dve.scalar_tensor_tensor(tok_b[:, :, :], sel[:, :, :], -1.0, tok_b[:, :, :], ALU.add, ALU.add))
            then(dve.tensor_reduce(ro_t[:, :], tok_b[:, :, :], AX.X, ALU.max))
            then(dve.tensor_scalar(ro_u[:, :], ro_t[:, :], 0.0, None, ALU.is_lt))
            then(dve.tensor_tensor(tok_c[:, :, :], prob[:, :, :], over_e(ro_u[:, :]), ALU.mult))
            then(dve.tensor_scalar(ro_u[:, :], ro_u[:, :], -1.0, None, ALU.add))
            then(dve.tensor_tensor(tok_c[:, :, :], tok_c[:, :, :], over_e(ro_u[:, :]), ALU.add))
            then(dve.tensor_tensor(tok_b[:, :, :], tok_b[:, :, :], tok_c[:, :, :], ALU.max))
            then(dve.tensor_reduce(weight[:, :], tok_b[:, :, :], AX.X, ALU.max))
            then(dve.tensor_tensor(tok_b[:, :, :], tok_b[:, :, :], over_e(weight[:, :]), ALU.is_equal))
            desc = cst[:, C_DESC:C_DESC + E].unsqueeze(1).broadcast_to([P, B, E])
            then(dve.tensor_tensor(tok_b[:, :, :], tok_b[:, :, :], desc, ALU.mult))
            then(dve.tensor_reduce(ro_t[:, :], tok_b[:, :, :], AX.X, ALU.max))
            onehot = tok_c
            then(dve.tensor_tensor(onehot[:, :, :], tok_b[:, :, :], over_e(ro_t[:, :]), ALU.is_equal))
            dve.tensor_copy(onehot_bf[:, :, :], onehot[:, :, :].rearrange("p t e -> p e t")).then_inc(found, 1)

            dve.wait_ge(ranked, 1)
            ends, totals = ex_b, ex_a
            then(dve.tensor_copy(totals[:, :], score_bank[2][:, :]))
            then(dve.tensor_tensor_scan(ends[:, :], cst[:, C_ONES:C_ONES + 1].broadcast_to([P, 512]),
                                        totals[:, :], 0.0, ALU.mult, ALU.add))
            then(dve.tensor_tensor(totals[:, :], ends[:, :], totals[:, :], ALU.subtract))
            start_e = totals[:, :].rearrange("p (e t) -> p e t", e=E)[:, :, 0]
            end_e = ends[:, :].rearrange("p (e t) -> p e t", e=E)[:, :, B - 1]
            then(dve.tensor_tensor(e_f[0][:, :], end_e, start_e, ALU.subtract))
            then(dve.tensor_scalar(e_f[0][:, :], e_f[0][:, :], float(P - 1), None, ALU.add))
            then(dve.tensor_copy(e_i[:, :], e_f[0][:, :]))
            then(dve.tensor_scalar(e_i2[:, :], e_i[:, :], 7, None, ALU.logical_shift_right))
            then(dve.tensor_copy(e_f[1][:, :], e_i2[:, :]))
            then(dve.tensor_tensor_scan(e_f[2][:, :], cst[:, C_ONES:C_ONES + E], e_f[1][:, :], 0.0,
                                        ALU.mult, ALU.add))
            then(dve.tensor_tensor(e_f[3][:, :], e_f[2][:, :], e_f[1][:, :], ALU.subtract))
            then(dve.scalar_tensor_tensor(e_f[4][:, :], e_f[3][:, :], float(P), start_e, ALU.mult, ALU.subtract))
            then(dve.tensor_tensor(tile_cmp[:, :, :],
                                   cst[:, C_TILE:C_TILE + NT].unsqueeze(2).broadcast_to([P, NT, E - 1]),
                                   e_f[2][:, 0:E - 1].unsqueeze(1).broadcast_to([P, NT, E - 1]), ALU.is_ge))
            then(dve.tensor_reduce(tile_e[:, :], tile_cmp[:, :, :], AX.X, ALU.add))
            dve.tensor_copy(tile_ei[:, :], tile_e[:, :]).then_inc(table_ready, 1)
            then(dve.tensor_tensor(totals[:, :], score_bank[1][:, :], totals[:, :], ALU.add))
            slots = ex_c[:, :].rearrange("p (e t) -> p e t", e=E)
            then(dve.tensor_tensor(slots, totals[:, :].rearrange("p (e t) -> p e t", e=E),
                                   e_f[4][:, :].unsqueeze(2).broadcast_to([P, E, B]), ALU.add))
            then(dve.tensor_tensor(tok_a[:, :, :], slots.rearrange("p e t -> p t e"), onehot[:, :, :], ALU.mult))
            then(dve.tensor_reduce(pos_f[:, :], tok_a[:, :, :], AX.X, ALU.add))
            dve.wait_ge(row_kept, B)
            then(dve.tensor_copy(rows[:, :, D], weight[:, :]))
            then(dve.tensor_copy(rows[:, :, D + 1], cst[:, C_TOK:C_TOK + B]))

            def stage(t, r):
                dve.tensor_copy(row_stage[r][:, :], rows[:, t, :]).then_inc(staged[r], 1)
                dve.tensor_copy(pos_stage[r][:, :], pos_f[:, bass.ds(t, 1)]).then_inc(staged[r], 1)

            for t in range(RS):
                stage(t, t)
            with dve.Fori(1, B // RS) as i:
                for r in range(RS):
                    dve.wait_ge(scattered[r], i * 16)
                    stage(i * RS + r, r)

            def hidden_rows(j):
                dve.wait_ge(hid_turned, j + 1)
                dve.tensor_copy(hid_t[:, :, :], value_bank[:, 0:F].rearrange("p (c t) -> p c t", c=2)).then_inc(hid_t_ready, 1)

            def ffn_norm(j, u4, stores):
                dve.wait_ge(y_made, j + 1)
                dve.scalar_tensor_tensor(y1[:, :], [tail_bank, proj_bank][u4 % 2][:, 0:D], xs[u4][:, D:D + 1], xs[u4][:, 0:D], ALU.mult,
                                         ALU.add).then_inc(y1_ready, 1)
                ge(dve, out_stored[u4], stores * 16)
                dve.tensor_copy(tok_i[u4][:, :], xs[u4][:, D + 1:D + 2]).then_inc(tok_ready, 1)
                dve.wait_ge(y1_ready, j + 1)
                dve.bn_stats(stats3[:, :], y1[:, :]).then_inc(st3_ready, 1)
                alone(dve)
                dve.wait_ge(st3_ready, j + 1)
                dve.bn_aggr(mv3[:, :], stats3[:, :]).then_inc(mv3_ready, 1)
                dve.wait_ge(rstd3_ready, j + 1)
                dve.tensor_scalar(y2[u4][:, :], y1[:, :], mv3[:, 0:1], rstd3[:, 0:1], ALU.subtract,
                                  ALU.mult).then_inc(y2_ready, 1)

            def ffn(j, u4, turn, first, last):
                if not first:
                    hidden_rows(j - 1)
                    ffn_norm(j - 1, (u4 - 1) % RS, turn(-1))

            tiles(dve, ffn)
            hidden_rows(NT - 1)
            ffn_norm(NT - 1, (NT - 1) % RS, (NT - 1) // RS)

        @block.scalar
        def _(act):
            for dst, src in ((cst[:, :], consts), (wq_sb[:, :], wq), (wk_sb[:, :], wk), (wv_sb[:, :], wv),
                             (wo_sb[:, :], wo), (bq_sb[:, :], bq), (bk_sb[:, :], bk), (sl_sb[:, :], slopes),
                             (bv_sb[:, :], bv), (bo_sb[:, :], bo), (wg_sb[:, :], wg),
                             (w1_sb[:, 0:4, :], w1[0:4].rearrange("e d f -> d e f")),
                             (w1_sb[:, 4:8, :], w1[4:8].rearrange("e d f -> d e f")),
                             (w2_sb[:, :, 0, :], w2[:, 0:P, :].rearrange("e f d -> f e d")),
                             (w2_sb[:, :, 1, :], w2[:, P:F, :].rearrange("e f d -> f e d"))):
                act.dma_start(dst, src).then_inc(weights_in, 16)

            def high_parts(n, u):
                act.wait_ge(qkv_made, n + 1)
                nc.scalar.activation(k_hi[:, :], proj_bank[:, 0:P], ACT.Identity, bias=bk_sb[:, 0:1])
                nc.scalar.activation(q_hi[:, :], proj_bank[:, P:2 * P], ACT.Identity, bias=bq_sb[:, 0:1])
                nc.scalar.activation(v_sb[u][:, :, HD:2 * HD],
                                     proj_bank[:, 2 * P:3 * P].rearrange("p (h d) -> p h d", h=H),
                                     ACT.Copy).then_inc(hi_ready, 1)

            def keep_keys(n, u):
                act.wait_ge(k_spread, n + 1)
                nc.scalar.activation(kt[u][:, :, :], proj_bank[:, :].rearrange("p (c t) -> p c t", c=NC_),
                                     ACT.Copy).then_inc(k_ready, 1)

            def keep_queries(n, u):
                act.wait_ge(q_spread, n + 1)
                nc.scalar.activation(qt[u][:, :, :], query_bank[:, :].rearrange("p (c t) -> p c t", c=NC_),
                                     ACT.Copy).then_inc(q_ready, 1)

            def keep_less_max(b):
                act.wait_ge(max_added, b + 1)
                nc.scalar.activation(q_less_max[:, :, :], query_bank[:, :].rearrange("p (c t) -> p c t", c=NC_),
                                     ACT.Copy).then_inc(qm_ready, 1)

            def keep_sums(p):
                act.wait_ge(summed, p + 1)
                nc.scalar.activation(sums[:, :, :], value_bank[:, 0:2 * P].rearrange("p (t q) -> p t q", t=2),
                                     ACT.Copy).then_inc(sums_ready, 1)

            def keep_x1t(p):
                act.wait_ge(x1_turned, p + 1)
                nc.scalar.activation(x1t[:, :], slot[1], ACT.Copy, scale=D ** -0.5).then_inc(x1t_ready, 1)

            def exp2(p):
                act.wait_ge(max2_ready, p + 1)
                nc.scalar.activation(p2[:, :], slot[2][:, 0:SK], ACT.Exp, bias=neg_max2[:, 0:1],
                                     accum_out=sum2[:, :]).then_inc(p2_ready, 1)

            def keep_p2t(p):
                act.wait_ge(p2_turned, p + 1)
                nc.scalar.activation(p2t[:, :], slot[3][0:SK, :], ACT.Copy).then_inc(p2t_ready, 1)

            def exp(b, g):
                act.wait_ge(rescored, 4 * b + g + 1)
                nc.scalar.activation(probs_t[:, g, :], score_bank[g][:, :], ACT.Exp).then_inc(probs_ready, 1)

            def keep_x2t(p):
                act.wait_ge(x2_turned, p + 1)
                nc.scalar.activation(x2t[:, :], slot[1], ACT.Copy).then_inc(x2t_ready, 1)

            act.wait_ge(prep, 2)
            high_parts(0, 0)
            keep_keys(0, 0)
            keep_queries(0, 0)

            def step(b, u, half, stages):
                proj, sco, val, tail = stages
                n, p, t, w = b + 1, b - 1, b - 2, 1 - u
                if tail:
                    keep_x1t(t)
                if val:
                    keep_sums(p)
                if tail:
                    exp2(t)
                if proj:
                    high_parts(n, w)
                if sco:
                    keep_less_max(b)
                if tail:
                    keep_p2t(t)
                if proj:
                    keep_keys(n, w)
                if sco:
                    for g in range(NG):
                        exp(b, g)
                if proj:
                    keep_queries(n, w)
                if tail:
                    keep_x2t(t)

            batches(act, step)

            act.wait_ge(gate_max_ready, 1)
            nc.scalar.activation(tok_b[:, :, :], tok_a[:, :, :], ACT.Exp).then_inc(gate_exp, 1)

            def keep_rows_t(j, u2):
                act.wait_ge(xs_turned, j + 1)
                nc.scalar.activation(xs_t[u2][:, :], score_bank[0][:, 0:P], ACT.Copy).then_inc(xs_t_ready, 1)

            def gelu(j, u2):
                act.wait_ge(hid_made, j + 1)
                nc.scalar.activation(hid[u2][:, :], score_bank[2 + u2][:, 0:F], ACT.Gelu).then_inc(hid_ready, 1)

            keep_rows_t(0, 0)

            def ffn(j, u4, turn, first, last):
                u2 = u4 % 2
                gelu(j, u2)
                if not last:
                    keep_rows_t(j + 1, 1 - u2)

            tiles(act, ffn)

        @block.gpsimd
        def _(pool):
            pool.memset(blank_row[:, 0:ROW - 1], 0.0).then_inc(blank_made, 1)
            pool.memset(blank_row[:, ROW - 1:ROW], float(2 * T)).then_inc(blank_made, 1)
            pool.memset(neg_half[:, :], -0.5).then_inc(blank_made, 1)
            pool.memset(eps[:, :], EPS).then_inc(blank_made, 1)
            pool.wait_ge(blank_made, 4)
            with pool.Fori(0, NT) as i:
                pool.dma_start(sorted_rows[bass.ts(i, P), :], blank_row[:, :]).then_inc(blanks_out, 16)

            def rstd(mv, ve, r, have, mid, done, n):
                pool.wait_ge(have, n)
                pool.tensor_tensor(ve[:, :], mv[:, 1:2], eps[:, :], ALU.add).then_inc(mid, 1)
                pool.wait_ge(mid, n)
                pool.tensor_tensor(r[:, :], ve[:, :], neg_half[:, :], ALU.pow).then_inc(done, 1)

            def add_bias(b, u, loads):
                pool.wait_ge(back_in[u], loads * 48)
                pool.tensor_tensor(x_plus_bias[u][:, :], x_sb[u][:, :], out_bias[:, :], ALU.add).then_inc(xb_ready, 1)

            def keep_row(p):
                alone(pool)
                pool.wait_ge(x2_ready, p + 1)
                pool.tensor_copy(rows[:, p, 0:D], x2[:, :]).then_inc(row_kept, 1)

            pool.wait_ge(weights_in, N_WEIGHTS)
            pool.wait_ge(prep, 3)

            def step(b, u, half, stages):
                proj, sco, val, tail = stages
                p, t = b - 1, b - 2
                if tail:
                    rstd(mv1, ve1, rstd1, mv1_ready, ve1_ready, rstd1_ready, t + 1)
                if val:
                    add_bias(p, 1 - u, half(-1) + 1)
                if tail:
                    rstd(mv2, ve2, rstd2, mv2_ready, ve2_ready, rstd2_ready, t + 1)
                    keep_row(t)

            batches(pool, step)

            pool.wait_ge(blanks_out, 16 * NT)
            last_slot = pool.to_reg(NT * P - 1)
            with pool.Fori(2, 2 * (B // RS) + 2, 2) as both:
                for r in range(RS):
                    alone(pool)
                    pool.wait_ge(staged[r], both)
                    pool.indirect_dma_start(out=sorted_rows[:, :],
                                            out_offset=bass.IndirectOffsetOnAxis(ap=pos_stage[r][:, 0:1], axis=0),
                                            in_=row_stage[r][:, :], in_offset=None, bounds_check=last_slot,
                                            oob_is_err=False).then_inc(scattered[r], 16)

            last_token = pool.to_reg(T - 1)

            def finish(j, u4):
                rstd(mv3, ve3, rstd3, mv3_ready, ve3_ready, rstd3_ready, j + 1)
                alone(pool)
                pool.wait_ge(y2_ready, j + 1)
                pool.wait_ge(tok_ready, j + 1)
                pool.indirect_dma_start(out=out, out_offset=bass.IndirectOffsetOnAxis(ap=tok_i[u4][:, 0:1], axis=0),
                                        in_=y2[u4][:, :], in_offset=None, bounds_check=last_token,
                                        oob_is_err=False).then_inc(out_stored[u4], 16)

            with pool.Fori(0, NT // RS) as i:
                for u in range(RS):
                    finish(i * RS + u, u)
            for u in range(RS):
                pool.wait_ge(out_stored[u], 16 * (NT // RS))


def constants():
    c = np.zeros((P, C_N), np.float32)
    p = np.arange(P)
    row = p % 32
    c[:, C_ID:C_ID + P] = np.eye(P)
    c[:, C_TQ:C_TQ + P] = np.where(((row == POS_ROW) | (row == POS_ROW + 1))[:, None], -p[None, :], 1)
    c[:, C_KAUG:C_KAUG + P] = np.where(((row == SLOPE_ROW) | (row == SLOPE_ROW + 1))[:, None], p[None, :],
                                       ((row >= POS_ROW) & (row < MAX_ROW + 2))[:, None])
    c[:, C_LOW] = (row == SLOPE_ROW + 1) | (row == POS_ROW + 1)
    g, r = p // 32, p % HD
    third = row // HD
    for base, thirds in ((C_QH, (0, 1)), (C_QL, (2,)), (C_KH, (0, 2)), (C_KL, (1,))):
        for t in range(NC_):
            c[32 * g + HD * t + r, base + P * t + p] = np.isin(third, thirds)
    for base, up in ((C_V, 0), (C_D, 2 * HD)):
        for t in range(2):
            mine = row // (2 * HD) == t
            c[(32 * g + up + row % (2 * HD))[mine], base + P * t + p[mine]] = 1
    same = p[:, None] % E == p[None, :] % E
    c[:, C_SAME:C_SAME + P] = same
    c[:, C_BELOW:C_BELOW + P] = same & (p[:, None] < p[None, :])
    c[:, C_TRI:C_TRI + P] = p[:, None] < p[None, :]
    c[:, C_DESC:C_DESC + E] = E - np.arange(E)
    c[:, C_TILE:C_TILE + NT] = np.arange(NT)
    c[:, C_ONES:C_ONES + P] = 1
    c[:, C_TOK:C_TOK + T // P] = p[:, None] + P * np.arange(T // P)[None, :]
    return c


def kernel(**inputs):
    import concourse.bacc as bacc
    from concourse.bass_utils import run_bass_kernel_spmd

    a = {k: np.asarray(v) for k, v in inputs.items()}
    x, ctx = a["x"], a["ctx_1024"]
    slopes = np.zeros((NG, 32, NC_), np.float32)
    slopes[:, SLOPE_ROW:POS_ROW + 2] = a["L0_attn_slopes"].reshape(NG, 1, NC_)
    arrays = {
        "x": x, "xt": x.transpose(0, 2, 1), "ctx": ctx, "ctxt": ctx.transpose(0, 2, 1),
        "wq": a["L0_attn_Wq"].T, "wk": a["L0_attn_Wk"].T, "wv": a["L0_attn_Wv"].T, "wo": a["L0_attn_Wo"].T,
        "bq": a["L0_attn_bq"].reshape(P, 1), "bk": a["L0_attn_bk"].reshape(P, 1), "slopes": slopes.reshape(P, NC_),
        "bv": a["L0_attn_bv"].reshape(P, 1), "bo": a["L0_attn_bo"].reshape(1, P),
        "wg": a["L0_ffn_Wg"], "w1": a["L0_ffn_W1"], "w2": a["L0_ffn_W2"], "consts": constants(),
    }
    nc = bacc.Bacc("TRN2", target_bir_lowering=False, num_devices=1)
    arrays = {f"in_{k}": np.ascontiguousarray(v) for k, v in arrays.items()}
    args = [nc.dram_tensor(k, v.shape, mybir.dt.from_np(v.dtype), kind="ExternalInput").ap() for k, v in arrays.items()]
    result = nc.dram_tensor("result", (T, D), F32, kind="ExternalOutput").ap()
    attention_ffn(nc, *args, result)
    r = run_bass_kernel_spmd(nc, [arrays], core_ids=[0])
    return r.results[0]["result"].reshape(B, S, D)
```

```python
from contextlib import ExitStack

import numpy as np

import concourse.bass as bass
from concourse import mybir

ACT = mybir.ActivationFunctionType
ALU = mybir.AluOpType
AX = mybir.AxisListType
F32 = mybir.dt.float32
BF16 = mybir.dt.bfloat16
I32 = mybir.dt.int32
F32R = mybir.dt.float32r

P = 128
B, S, D = 64, 128, 128
SK = 120
H, HD = 16, 8
NG, NC_ = 4, 4
E, F = 8, 256
T = B * S
CAP = max(1, T // E)
NT = T // P + E
ROW = D + 2
EPS = 1e-5
ORDER = (3, 0, 1, 2)
PROB_BITS = 30
SLOPE_ROW, POS_ROW, MAX_ROW, BIAS_ROW = 3 * HD, 3 * HD + 2, 3 * HD + 4, 3 * HD + 6
VW = 5 * HD

C_ID, C_TQ, C_KAUG, C_SAME, C_BELOW, C_TRI = (i * P for i in range(6))
C_ROWS = 6 * P
C_BIAS = C_ROWS + P
C_V, C_D = (C_BIAS + NC_ * P + i * 2 * P for i in range(2))
C_DESC = C_D + 2 * P
C_TILE = C_DESC + E
C_ONES = C_TILE + NT
C_LOW = C_ONES + P
C_TOK = C_LOW + 4
C_DIGIT = C_TOK + T // P
C_N = C_DIGIT + 8


def attention_ffn(nc, x, xt, ctx_in, ctxt, wq, wk, wv, wo, bq, bk, slopes, bv, bo, wg, w1, w2, consts, out):
    st = ExitStack()
    with st:
        def sb(name, shape, dt=F32):
            return st.enter_context(nc.sbuf_tensor(name, shape, dt))

        def bank(name):
            return st.enter_context(nc.psum_tensor(name, [P, 512], F32))

        def sem(name):
            return st.enter_context(nc.semaphore(name))

        sorted_rows = nc.dram_tensor("sorted_rows", [NT * P, ROW], F32, kind="Internal").ap()

        cst = sb("cst", [P, C_N])
        ident = cst[:, C_ID:C_ID + P]
        wq_sb, wk_sb = (sb(n, [P, NC_, P]) for n in ("wq_sb", "wk_sb"))
        wv_sb, wo_sb = (sb(n, [P, P]) for n in ("wv_sb", "wo_sb"))
        wg_sb = sb("wg_sb", [P, E])
        w1_sb, w2_sb = sb("w1_sb", [P, E, F]), sb("w2_sb", [P, E, 2, D])
        bq_sb, bk_sb, sl_sb = sb("bq_sb", [P, P]), sb("bk_sb", [P, P]), sb("sl_sb", [P, NC_])
        bv_sb, bo_sb = sb("bv_sb", [P, 1]), sb("bo_sb", [1, P])
        ident_r, minus_ident = sb("ident_r", [P, P], F32R), sb("minus_ident", [P, P], F32R)
        add_to_q, add_to_k, add_h = (sb(n, [P, P], F32R) for n in ("add_to_q", "add_to_k", "add_h"))
        q_rows_added, k_rows_added = sb("q_rows_added", [P, NC_, P], F32R), sb("k_rows_added", [P, NC_, P], F32R)
        aug, aug_h = sb("aug", [P, NC_, P]), sb("aug_h", [P, NC_, P], F32R)
        bv_wide, out_bias = sb("bv_wide", [P, P]), sb("out_bias", [P, P])
        tri_bf, ones_bf = sb("tri_bf", [P, P], BF16), sb("ones_bf", [P, P], BF16)
        neg_half, eps = sb("neg_half", [P, 4]), sb("eps", [P, 4])
        blank_row = sb("blank_row", [P, ROW])

        xt_sb = [sb(f"xt_sb{u}", [P, P]) for u in range(2)]
        x_sb = [sb(f"x_sb{u}", [P, P]) for u in range(2)]
        c_sb = [sb(f"c_sb{u}", [SK, P]) for u in range(2)]
        ct_sb = [sb(f"ct_sb{u}", [P, SK]) for u in range(2)]
        x_plus_bias = [sb(f"x_plus_bias{u}", [P, P]) for u in range(2)]
        q_high, k_high = (sb(n, [P, NC_, P], F32R) for n in ("q_high", "k_high"))
        qt = [sb(f"qt{u}", [P, NC_, P], F32R) for u in range(2)]
        kt = [sb(f"kt{u}", [P, NC_, P], F32R) for u in range(2)]
        v_sb = [sb(f"v_sb{u}", [P, H, VW]) for u in range(2)]
        q_less_max = sb("q_less_max", [P, NC_, P], F32R)
        neg_max = sb("neg_max", [P, NG, NC_])
        max_rows = sb("max_rows", [P, NC_, P], F32R)
        probs_t = sb("probs_t", [P, NG, 512])
        sums = sb("sums", [P, 2, P])
        den_rec, heads_out = sb("den_rec", [P, P]), sb("heads_out", [P, P])
        t1, t2, x2 = (sb(n, [P, P]) for n in ("t1", "t2", "x2"))
        x1 = [sb(f"x1_{u}", [P, P]) for u in range(2)]
        x1t, x2t, p2, p2t = sb("x1t", [P, P]), sb("x2t", [P, P]), sb("p2", [P, SK]), sb("p2t", [SK, P])
        stats1, stats2 = sb("stats1", [P, 6]), sb("stats2", [P, 6])
        mv1, mv2 = sb("mv1", [P, 2]), sb("mv2", [P, 2])
        ve1, ve2, rstd1, rstd2 = (sb(n, [P, 1]) for n in ("ve1", "ve2", "rstd1", "rstd2"))
        neg_max2, sum2, rec2 = (sb(n, [P, 1]) for n in ("neg_max2", "sum2", "rec2"))
        rows = sb("rows", [P, B, ROW])

        proj_bank, query_bank, value_bank, tail_bank = (
            bank(n) for n in ("proj_bank", "query_bank", "value_bank", "tail_bank"))
        score_bank = [bank(f"score_bank{g}") for g in range(NG)]
        slot = [tail_bank[:, i * P:(i + 1) * P] for i in range(4)]

        logits = sb("logits", [P, B, E])
        tok_a, tok_b, tok_c, prob = (sb(n, [P, B, E]) for n in ("tok_a", "tok_b", "tok_c", "prob"))
        ro_t, ro_u, weight = sb("ro_t", [P, B]), sb("ro_u", [P, B]), sb("weight", [P, B])
        prob_e, ex_a, ex_b, ex_c = (sb(n, [P, 512]) for n in ("prob_e", "ex_a", "ex_b", "ex_c"))
        cand, cnt, keep = sb("cand", [P, 3]), sb("cnt", [P, 3]), sb("keep", [P, 4])
        thr = keep[:, 3:4]
        two_bits = sb("two_bits", [P, 3], I32)
        need, before = sb("need", [P, 1]), sb("before", [P, 1])
        onehot_bf = sb("onehot_bf", [P, E, B], BF16)
        e_f = [sb(f"e_f{i}", [P, E]) for i in range(5)]
        e_i, e_i2 = sb("e_i", [P, E], I32), sb("e_i2", [P, E], I32)
        tile_cmp = sb("tile_cmp", [P, NT, E - 1])
        NW = NT // 8
        tile_e, tile_i = sb("tile_e", [P, 8 * NW + 8]), sb("tile_i", [P, 8 * NW + 8], I32)
        low_digits, words = sb("low_digits", [P, NW]), [sb(f"words{i}", [P, NW], I32) for i in range(5)]
        pos_f = sb("pos_f", [P, B])

        RS = 4
        row_stage = [sb(f"row_stage{i}", [P, ROW]) for i in range(RS)]
        pos_stage = [sb(f"pos_stage{i}", [P, 1], I32) for i in range(RS)]
        xs = [sb(f"xs{i}", [P, ROW]) for i in range(8)]
        xs_t = [sb(f"xs_t{i}", [P, P]) for i in range(2)]
        hid = [sb(f"hid{i}", [P, F]) for i in range(2)]
        hid_t = [sb(f"hid_t{i}", [P, 2, P]) for i in range(2)]
        y1 = [sb(f"y1_{i}", [P, P]) for i in range(8)]
        y2 = [sb(f"y2_{i}", [P, P]) for i in range(8)]
        tok_i = [sb(f"tok_i{i}", [P, 1], I32) for i in range(8)]
        stats3 = [sb(f"stats3_{i}", [P, 6]) for i in range(2)]
        mv3, ve3, rstd3 = sb("mv3", [P, 8, 2]), sb("ve3", [P, 8]), sb("rstd3", [P, 8])

        names = """weights_in ffn_weights_in prep blank_made front_in0 front_in1 back_in0 back_in1 context_in0 context_in1 blanks_out
        v_made k_made q_made k_split q_split scored max_added rescored summed compacted projected x1_turned scored2 p2_turned
        attended2 x2_turned gated bias_made
        k_high_ready q_high_ready k_ready q_ready max_ready max_hi_ready max_lo_ready qm_ready sums_ready den_ready heads_ready t1_ready st1_ready mv1_ready x1_ready
        max2_ready rec2_ready t2_ready st2_ready mv2_ready x2_ready logits_ready
        x1t_ready p2_ready v_ready p2t_ready probs_ready x2t_ready
        xb_ready ve1_ready rstd1_ready ve2_ready rstd2_ready row_kept
        dve_step gate_max_ready gate_exp gates_turned counted sel_turned ranked found searched bit_ready
        table_ready staged0 staged1 staged2 staged3 scattered0 scattered1 scattered2 scattered3 xs_in0 xs_in1 xs_in2 xs_in3 xs_in4 xs_in5 xs_in6 xs_in7
        xs_turned xs_t_ready hid_made hid_ready hid_turned hid_t_ready y_made y1_ready st3_ready mv3_ready ve3_ready
        rstd3_ready y2_ready0 y2_ready1 y2_ready2 y2_ready3 y2_ready4 y2_ready5 y2_ready6 y2_ready7 tok_ready out_stored0 out_stored1 out_stored2 out_stored3 out_stored4 out_stored5 out_stored6 out_stored7""".split()
        s = {n: sem(n) for n in names}
        (weights_in, ffn_weights_in, prep, blank_made, front_in0, front_in1, back_in0, back_in1, context_in0, context_in1, blanks_out,
         v_made, k_made, q_made, k_split, q_split, scored, max_added, rescored, summed, compacted, projected, x1_turned, scored2,
         p2_turned,
         attended2, x2_turned, gated, bias_made,
         k_high_ready, q_high_ready, k_ready, q_ready, max_ready, max_hi_ready, max_lo_ready, qm_ready, sums_ready, den_ready, heads_ready, t1_ready, st1_ready, mv1_ready, x1_ready,
         max2_ready, rec2_ready, t2_ready, st2_ready, mv2_ready, x2_ready, logits_ready,
         x1t_ready, p2_ready, v_ready, p2t_ready, probs_ready, x2t_ready,
         xb_ready, ve1_ready, rstd1_ready, ve2_ready, rstd2_ready, row_kept,
         dve_step, gate_max_ready, gate_exp, gates_turned, counted, sel_turned, ranked, found, searched, bit_ready,
         table_ready, staged0, staged1, staged2, staged3, scattered0, scattered1, scattered2, scattered3,
         xs_in0, xs_in1, xs_in2, xs_in3, xs_in4, xs_in5, xs_in6, xs_in7,
         xs_turned, xs_t_ready, hid_made, hid_ready, hid_turned, hid_t_ready, y_made, y1_ready, st3_ready, mv3_ready,
         ve3_ready, rstd3_ready, y2_ready0, y2_ready1, y2_ready2, y2_ready3, y2_ready4, y2_ready5, y2_ready6, y2_ready7, tok_ready, out_stored0, out_stored1, out_stored2, out_stored3,
         out_stored4, out_stored5, out_stored6, out_stored7) = (s[n] for n in names)
        front_in, back_in, ctx_in_sb = [front_in0, front_in1], [back_in0, back_in1], [context_in0, context_in1]
        staged = [staged0, staged1, staged2, staged3]
        scattered = [scattered0, scattered1, scattered2, scattered3]
        xs_in = [xs_in0, xs_in1, xs_in2, xs_in3, xs_in4, xs_in5, xs_in6, xs_in7]
        y2_ready = [y2_ready0, y2_ready1, y2_ready2, y2_ready3, y2_ready4, y2_ready5, y2_ready6, y2_ready7]
        out_stored = [out_stored0, out_stored1, out_stored2, out_stored3, out_stored4, out_stored5, out_stored6, out_stored7]
        N_WEIGHTS = 11 * 16
        BLANK_PARTS = 8

        def ge(eng, semaphore, value):
            if not (isinstance(value, int) and value <= 0):
                eng.wait_ge(semaphore, value)

        def alone(eng):
            eng.wait_ge(weights_in, N_WEIGHTS)

        def batches(eng, step):
            def peeled(b):
                step(b, b % 2, lambda d: (b + d) // 2,
                     (b + 1 < B, b < B, 1 <= b <= B, 2 <= b <= B + 1, b >= 3))

            for b in range(3):
                peeled(b)
            with eng.Fori(0, (B - 4) // 2) as i:
                for u in range(2):
                    step(i * 2 + (3 + u), (3 + u) % 2, lambda d: i + (3 + u + d) // 2, (True,) * 5)
            for b in range(B - 1, B + 3):
                peeled(b)

        def tiles(eng, step, lead, before=None):
            def written_out(first):
                if before:
                    before(first // 8)
                for j in range(first, first + 8):
                    step(j, j % 8, lambda d: (j + d) // 4, j // 8)

            for o in range(lead):
                written_out(8 * o)
            with eng.Fori(0, NT // 8 - 1 - lead) as i:
                if before:
                    before(i + lead)
                for v in range(8):
                    step(i * 8 + (8 * lead + v), v, lambda d: i * 2 + (8 * lead + v + d) // 4,
                         i + lead)
            written_out(NT - 8)

        ht_bank, y_bank = [value_bank, query_bank], [tail_bank, proj_bank]

        block = st.enter_context(nc.Block())

        @block.sync
        def _(sp):
            def front(n, u):
                sp.dma_start(xt_sb[u][:, :], xt[n]).then_inc(front_in[u], 16)

            def back(n, u):
                sp.dma_start(x_sb[u][:, :], x[n]).then_inc(back_in[u], 16)

            def context(n, u):
                sp.dma_start(ct_sb[u][:, :], ctxt[n]).then_inc(ctx_in_sb[u], 16)
                sp.dma_start(c_sb[u][:, :], ctx_in[n]).then_inc(ctx_in_sb[u], 16)

            def turn(b, u, has_front, has_back, has_rows):
                if has_front:
                    sp.wait_ge(q_made, b + 1)
                    front(b + 2, u)
                if has_back:
                    sp.wait_ge(xb_ready, b - 1)
                    back(b, u)
                if has_rows:
                    sp.wait_ge(attended2, b - 2)
                    context(b - 1, 1 - u)

            front(0, 0)
            front(1, 1)
            for n in range(2):
                back(n, n)
                context(n, n)

            def peeled(b):
                turn(b, b % 2, b + 2 < B, 2 <= b < B, b >= 3)

            for b in range(4):
                peeled(b)
            with sp.Fori(0, (B - 6) // 2) as i:
                for u in range(2):
                    turn(i * 2 + (4 + u), u, True, True, True)
            for b in range(B - 2, B + 1):
                peeled(b)

            for r in range(RS):
                sp.wait_ge(scattered[r], 16 * (B // RS))

            def load_rows(j, u):
                sp.dma_start(xs[u][:, :], sorted_rows[bass.ts(j, P), :]).then_inc(xs_in[u], 16)

            for j in range(8):
                load_rows(j, j)
            with sp.Fori(0, NT // 8 - 1) as i:
                for v in range(8):
                    j = i * 8 + v
                    sp.wait_ge(tok_ready, j + 1)
                    load_rows(j + 8, v)

        @block.tensor
        def _(pe):
            def project_values(n, u, loads):
                pe.wait_ge(front_in[u], loads * 16)
                ge(pe, v_ready, n)
                pe.matmul(value_bank[:, 2 * P:3 * P], xt_sb[u][:, :], wv_sb[:, :], start=True,
                          stop=True).then_inc(v_made, 1)

            def project_rows(dst, u, weights, add, added):
                for c in range(NC_):
                    pe.matmul(dst[:, c * P:(c + 1) * P], weights[:, c, :], xt_sb[u][:, :], start=(c == 0),
                              stop=False, skip_group_check=True)
                return pe.matmul(dst[:, :], add[:, :], added[:, :, :], start=False, stop=True,
                                 skip_group_check=True)

            def project_keys(n, u):
                ge(pe, k_ready, n)
                project_rows(proj_bank, u, wk_sb, add_to_k, k_rows_added).then_inc(k_made, 1)

            def project_queries(n, u):
                ge(pe, qm_ready, n)
                project_rows(query_bank, u, wq_sb, add_to_q, q_rows_added).then_inc(q_made, 1)

            def split_keys(n):
                pe.wait_ge(k_high_ready, n + 1)
                pe.matmul(proj_bank[:, :], minus_ident[:, :], k_high[:, :, :], start=False, stop=True,
                          skip_group_check=True).then_inc(k_split, 1)

            def split_queries(n):
                pe.wait_ge(q_high_ready, n + 1)
                pe.matmul(query_bank[:, :], minus_ident[:, :], q_high[:, :, :], start=False, stop=True,
                          skip_group_check=True).then_inc(q_split, 1)

            def score(b, u, *groups):
                if groups[0] == 0:
                    pe.wait_ge(k_ready, b + 1)
                    pe.wait_ge(q_ready, b + 1)
                ge(pe, probs_ready, 4 * b - 3 + max(ORDER.index(g) for g in groups))
                if 3 in groups and not (isinstance(b, int) and b < 2):
                    pe.wait_ge(heads_ready, b - 1)
                for c in range(NC_):
                    for g in groups:
                        r = slice(32 * g, 32 * g + 32)
                        mm = pe.matmul(score_bank[g][:, c * P:(c + 1) * P], qt[u][r, c, :], kt[u][r, c, :],
                                       start=True, stop=True, tile_position=(32 * g, 0))
                        if c == NC_ - 1:
                            mm.then_inc(scored, 1)

            def add_max(b):
                pe.wait_ge(max_lo_ready, b + 1)
                for c in range(NC_):
                    mm = pe.matmul(query_bank[:, c * P:(c + 1) * P], max_rows[:, c, :], ident_r[:, :], start=False,
                                   stop=True, skip_group_check=True)
                mm.then_inc(max_added, 1)

            def rescore(b, u, *groups):
                if groups[0] == ORDER[0]:
                    pe.wait_ge(qm_ready, b + 1)
                for c in range(NC_):
                    for g in groups:
                        r = slice(32 * g, 32 * g + 32)
                        mm = pe.matmul(score_bank[g][:, c * P:(c + 1) * P], kt[u][r, c, :], q_less_max[r, c, :],
                                       start=True, stop=True, tile_position=(32 * g, 0))
                        if c == NC_ - 1:
                            mm.then_inc(rescored, 1)

            def sum_values(p, u, half_of_tiles):
                pe.wait_ge(probs_ready, 4 * p + 4)
                pe.wait_ge(v_ready, p + 1)
                for c in (2 * half_of_tiles, 2 * half_of_tiles + 1):
                    w = slice(HD, VW) if c % 2 == 0 else slice(0, VW - HD)
                    q = slice((c // 2) * P, (c // 2 + 1) * P)
                    for g in range(NG):
                        r = slice(32 * g, 32 * g + 32)
                        mm = pe.matmul(value_bank[r, q], v_sb[u][:, NC_ * g + c, w],
                                       probs_t[:, g, c * P:(c + 1) * P], start=(c % 2 == 0), stop=(c % 2 == 1),
                                       tile_position=(0, 32 * g))
                if half_of_tiles == 1:
                    mm.then_inc(summed, 1)

            def compact(p, b):
                pe.wait_ge(sums_ready, p + 1)
                pe.wait_ge(probs_ready, min(4 * b + 1, 4 * B) if isinstance(b, int) else 4 * b + 1)
                for i, base in enumerate((C_V, C_D)):
                    for j in range(2):
                        mm = pe.matmul(score_bank[3][:, i * P:(i + 1) * P], cst[:, base + j * P:base + (j + 1) * P],
                                       sums[:, j, :], start=(j == 0), stop=(j == 1))
                mm.then_inc(compacted, 1)

            def score2(e, u, loads, last):
                pe.wait_ge(ctx_in_sb[u], loads * 32)
                pe.wait_ge(x1t_ready, e + 1)
                if last:
                    pe.wait_ge(logits_ready, e)
                pe.matmul(slot[0][:, 0:SK], x1t[:, :], ct_sb[u][:, :], start=True, stop=True).then_inc(scored2, 1)

            def turn_p2(e):
                pe.wait_ge(p2_ready, e + 1)
                pe.transpose(slot[1][0:SK, :], p2[:, :], ident).then_inc(p2_turned, 1)

            def attend2(e, u):
                pe.wait_ge(p2t_ready, e + 1)
                pe.matmul(slot[2], p2t[:, :], c_sb[u][:, :], start=True, stop=True).then_inc(attended2, 1)

            def project_out(t, end):
                pe.wait_ge(heads_ready, t + 1)
                if end:
                    pe.wait_ge(t2_ready, t)
                pe.matmul(slot[3], heads_out[:, :], wo_sb[:, :], start=True, stop=True).then_inc(projected, 1)

            def turn_x2(e, tail):
                pe.wait_ge(x2_ready, e + 1)
                if tail:
                    pe.wait_ge(t1_ready, e + 2)
                pe.transpose(slot[0], x2[:, :], ident).then_inc(x2_turned, 1)

            def turn_x1(t, u, end):
                pe.wait_ge(x1_ready, t + 1)
                if end:
                    pe.wait_ge(logits_ready, t)
                pe.transpose(slot[1], x1[u][:, :], ident).then_inc(x1_turned, 1)

            def gate(e):
                pe.wait_ge(x2t_ready, e + 1)
                pe.matmul(slot[2][:, 0:E], x2t[:, :], wg_sb[:, :], start=True, stop=True).then_inc(gated, 1)

            pe.wait_ge(weights_in, N_WEIGHTS)
            pe.wait_ge(prep, 1)
            pe.matmul(slot[0], bv_wide[:, :], wo_sb[:, :], start=True, stop=False)
            pe.matmul(slot[0], cst[0:1, C_ONES:C_ONES + P], bo_sb[:, :], start=False, stop=True).then_inc(bias_made, 1)
            pe.wait_ge(prep, 2)
            project_values(0, 0, 1)
            project_keys(0, 0)
            project_queries(0, 0)
            split_keys(0)
            split_queries(0)

            def step(b, u, half, stages):
                proj, sco, val, tail, end = stages
                n, p, t, e, w = b + 1, b - 1, b - 2, b - 3, 1 - u
                if end:
                    score2(e, w, half(-3) + 1, not tail)
                if proj:
                    project_values(n, w, half(1) + 1)
                if sco:
                    score(b, u, 0)
                    score(b, u, 1)
                if val:
                    sum_values(p, w, 0)
                if end:
                    turn_p2(e)
                if sco:
                    score(b, u, 2, 3)
                if end:
                    attend2(e, w)
                if proj:
                    project_keys(n, w)
                if val:
                    sum_values(p, w, 1)
                if tail:
                    project_out(t, end)
                if sco:
                    add_max(b)
                if proj:
                    split_keys(n)
                    project_queries(n, w)
                if end:
                    turn_x2(e, tail)
                if sco:
                    rescore(b, u, ORDER[0], ORDER[1])
                if end:
                    gate(e)
                if sco:
                    rescore(b, u, ORDER[2])
                if proj:
                    split_queries(n)
                if tail:
                    turn_x1(t, u, end)
                if val:
                    compact(p, b)
                if sco:
                    rescore(b, u, ORDER[3])

            batches(pe, step)

            pe.wait_ge(found, 1)
            for b4 in range(4):
                mm = pe.transpose(score_bank[0][:, b4 * P:(b4 + 1) * P], ex_b[:, b4 * P:(b4 + 1) * P], ident)
            mm.then_inc(gates_turned, 1)

            def count(n, rhs, weights, dst):
                pe.wait_ge(searched, n)
                pe.matmul(dst, weights, rhs, start=True, stop=True).then_inc(counted, 1)

            same = cst[:, C_SAME:C_SAME + P]
            with pe.Fori(3, PROB_BITS // 2 * 3 + 3, 3) as n:
                count(n, cnt[:, :], same, score_bank[1][:, 0:3])
            count(PROB_BITS // 2 * 3 + 1, cnt[:, 0:1], same, score_bank[1][:, 0:1])
            count(PROB_BITS // 2 * 3 + 2, cnt[:, 1:2], cst[:, C_BELOW:C_BELOW + P], score_bank[1][:, 1:2])
            pe.wait_ge(found, 2)
            for b4 in range(4):
                mm = pe.transpose(score_bank[0][:, b4 * P:(b4 + 1) * P], ex_a[:, b4 * P:(b4 + 1) * P], ident)
            mm.then_inc(sel_turned, 1)
            pe.wait_ge(found, 3)
            pe.matmul(score_bank[1][:, :], tri_bf[:, :], onehot_bf[:, :, :], start=True, stop=True)
            pe.matmul(score_bank[2][:, :], ones_bf[:, :], onehot_bf[:, :, :], start=True, stop=True).then_inc(ranked, 1)

            rows_bank, h_bank = [score_bank[0], score_bank[1]], [score_bank[2], score_bank[3]]

            def turn_rows(j, v, loads):
                pe.wait_ge(xs_in[v], loads * 16)
                ge(pe, xs_t_ready, j - 1)
                pe.transpose(rows_bank[v % 2][:, 0:P], xs[v][:, 0:D], ident).then_inc(xs_turned, 1)

            def hidden(j, u2, e):
                pe.wait_ge(xs_t_ready, j + 1)
                ge(pe, hid_ready, j - 1)
                pe.matmul(h_bank[u2][:, 0:F], xs_t[u2][:, :], w1_sb[:, e, :], start=True, stop=True).then_inc(hid_made, 1)

            def turn_hidden(j, u2):
                pe.wait_ge(hid_ready, j + 1)
                ge(pe, hid_t_ready, j - 1)
                pe.transpose(ht_bank[u2][:, 0:P], hid[u2][:, 0:P], ident)
                pe.transpose(ht_bank[u2][:, P:2 * P], hid[u2][:, P:2 * P], ident).then_inc(hid_turned, 1)

            def back_to_rows(j, u2, e):
                pe.wait_ge(hid_t_ready, j + 1)
                ge(pe, y1_ready, j - 1)
                pe.matmul(y_bank[u2][:, 0:D], hid_t[u2][:, 0, :], w2_sb[:, e, 0, :], start=True, stop=False)
                pe.matmul(y_bank[u2][:, 0:D], hid_t[u2][:, 1, :], w2_sb[:, e, 1, :], start=False, stop=True).then_inc(y_made, 1)

            experts = {}

            def load_experts(m):
                word = pe.value_load(words[4][0:1, bass.ds(m, 1)], min_val=0, max_val=8 ** 10 - 1)
                for d in range(-1, 9):
                    experts[d] = (word // 8 ** (d + 1)) % 8

            pe.wait_ge(ffn_weights_in, 4 * 16)
            pe.wait_ge(table_ready, 1)
            turn_rows(0, 0, 1)
            turn_rows(1, 1, 1)

            def ffn(j, v, four, eight):
                inside = not isinstance(j, int)
                if inside or j + 2 < NT:
                    turn_rows(j + 2, (v + 2) % 8, eight + (v + 2) // 8 + 1)
                if not inside and j == 0:
                    hidden(0, 0, experts[0])
                if inside or j + 1 < NT:
                    hidden(j + 1, (v + 1) % 2, experts[v + 1])
                turn_hidden(j, v % 2)
                if inside or j > 0:
                    back_to_rows(j - 1, (v + 1) % 2, experts[v - 1])

            tiles(pe, ffn, 1, load_experts)
            back_to_rows(NT - 1, (NT - 1) % 2, experts[7])

        @block.vector
        def _(dve):
            steps = [0]

            def then(ins):
                steps[0] += 1
                ins.then_inc(dve_step, 1)
                dve.wait_ge(dve_step, steps[0])

            for u in range(2):
                then(dve.memset(v_sb[u][:, :, :], 0.0))
                then(dve.memset(v_sb[u][:, :, 3 * HD:4 * HD], 1.0))
            then(dve.memset(max_rows[:, :, :].bitcast(F32), 0.0))
            dve.wait_ge(weights_in, N_WEIGHTS)
            then(dve.memset(bv_wide[:, :], 0.0))
            dve.tensor_scalar(bv_wide[:, :], bv_wide[:, :], bv_sb[:, 0:1], None, ALU.add).then_inc(prep, 1)
            then(dve.tensor_scalar(bq_sb[:, :], bq_sb[:, :], HD ** -0.5, None, ALU.mult))
            then(dve.tensor_copy(ident_r[:, :], ident))
            then(dve.tensor_scalar(minus_ident[:, :], ident, -1.0, None, ALU.mult))
            for bias, add in ((bq_sb, add_to_q), (bk_sb, add_to_k)):
                then(dve.tensor_tensor(bias[:, :], bias[:, :], cst[:, C_ROWS:C_ROWS + P], ALU.add))
                then(dve.tensor_scalar(add_h[:, :], bias[:, :], cst[:, C_LOW + 1:C_LOW + 2], None, ALU.mult))
                then(dve.tensor_tensor(add[:, :], bias[:, :], add_h[:, :].bitcast(F32), ALU.subtract))
            tiles_of_bias = cst[:, C_BIAS:C_BIAS + NC_ * P].rearrange("p (c t) -> p c t", c=NC_)
            then(dve.tensor_tensor(k_rows_added[:, :, :], tiles_of_bias,
                                   cst[:, C_KAUG:C_KAUG + P].unsqueeze(1).broadcast_to([P, NC_, P]), ALU.add))
            then(dve.tensor_tensor(aug[:, :, :], cst[:, C_TQ:C_TQ + P].unsqueeze(1).broadcast_to([P, NC_, P]),
                                   sl_sb[:, :].unsqueeze(2).broadcast_to([P, NC_, P]), ALU.mult))
            then(dve.tensor_tensor(aug[:, :, :], aug[:, :, :], tiles_of_bias, ALU.add))
            then(dve.tensor_scalar(aug_h[:, :, :], aug[:, :, :], cst[:, C_LOW:C_LOW + 1], None, ALU.mult))
            then(dve.tensor_tensor(q_rows_added[:, :, :], aug[:, :, :], aug_h[:, :, :].bitcast(F32), ALU.subtract))
            dve.tensor_scalar(wq_sb[:, :, :], wq_sb[:, :, :], HD ** -0.5, None, ALU.mult).then_inc(prep, 1)
            dve.wait_ge(bias_made, 1)
            dve.tensor_copy(out_bias[:, :], slot[0]).then_inc(prep, 1)
            dve.tensor_copy(tri_bf[:, :], cst[:, C_TRI:C_TRI + P])
            dve.memset(ones_bf[:, :], 1.0)

            def row_max(b, g):
                dve.wait_ge(scored, 4 * b + g + 1)
                dve.tensor_reduce(neg_max[:, g, :], score_bank[g][:, :].rearrange("p (c k) -> p c k", c=NC_),
                                  AX.X, ALU.max, negate=True).then_inc(max_ready, 1)

            max_view = max_rows[:, :, :].rearrange("p c (g r) -> p g c r", g=NG)

            def keep_max_high(b):
                dve.wait_ge(max_ready, 4 * b + 4)
                ge(dve, max_added, b)
                dve.tensor_copy(max_view[:, :, :, MAX_ROW], neg_max[:, :, :]).then_inc(max_hi_ready, 1)

            def keep_max_low(b):
                dve.wait_ge(max_hi_ready, b + 1)
                dve.tensor_tensor(max_view[:, :, :, MAX_ROW + 1], neg_max[:, :, :],
                                  max_view[:, :, :, MAX_ROW].bitcast(F32), ALU.subtract).then_inc(max_lo_ready, 1)

            def invert_sums(p):
                dve.wait_ge(compacted, p + 1)
                dve.reciprocal(den_rec[:, :], score_bank[3][:, P:2 * P]).then_inc(den_ready, 1)

            def normalise(p):
                dve.wait_ge(den_ready, p + 1)
                dve.tensor_tensor(heads_out[:, :], score_bank[3][:, 0:P], den_rec[:, :],
                                  ALU.mult).then_inc(heads_ready, 1)

            def residual1(p, u):
                dve.wait_ge(projected, p + 1)
                dve.wait_ge(xb_ready, p + 1)
                dve.tensor_tensor(t1[:, :], slot[3], x_plus_bias[u][:, :], ALU.add).then_inc(t1_ready, 1)

            def stats_of_t1(p):
                dve.wait_ge(t1_ready, p + 1)
                dve.bn_stats(stats1[:, :], t1[:, :]).then_inc(st1_ready, 1)

            def moments_of_t1(p):
                alone(dve)
                dve.wait_ge(st1_ready, p + 1)
                dve.bn_aggr(mv1[:, :], stats1[:, :]).then_inc(mv1_ready, 1)

            def norm1(p, u):
                dve.wait_ge(rstd1_ready, p + 1)
                dve.tensor_scalar(x1[u][:, :], t1[:, :], mv1[:, 0:1], rstd1[:, 0:1], ALU.subtract,
                                  ALU.mult).then_inc(x1_ready, 1)

            def row_max2(p):
                dve.wait_ge(scored2, p + 1)
                dve.tensor_reduce(neg_max2[:, :], slot[0][:, 0:SK], AX.X, ALU.max, negate=True).then_inc(max2_ready, 1)

            def invert_sum2(p):
                dve.wait_ge(p2_ready, p + 1)
                dve.reciprocal(rec2[:, :], sum2[:, :]).then_inc(rec2_ready, 1)

            def residual2(p, u):
                dve.wait_ge(rec2_ready, p + 1)
                dve.wait_ge(attended2, p + 1)
                dve.scalar_tensor_tensor(t2[:, :], slot[2], rec2[:, 0:1], x1[u][:, :], ALU.mult,
                                         ALU.add).then_inc(t2_ready, 1)

            def stats_of_t2(p):
                dve.wait_ge(t2_ready, p + 1)
                dve.bn_stats(stats2[:, :], t2[:, :]).then_inc(st2_ready, 1)

            def moments_of_t2(p):
                alone(dve)
                dve.wait_ge(st2_ready, p + 1)
                dve.bn_aggr(mv2[:, :], stats2[:, :]).then_inc(mv2_ready, 1)

            def norm2(p):
                dve.wait_ge(rstd2_ready, p + 1)
                dve.tensor_scalar(x2[:, :], t2[:, :], mv2[:, 0:1], rstd2[:, 0:1], ALU.subtract,
                                  ALU.mult).then_inc(x2_ready, 1)

            def keep_logits(p):
                dve.wait_ge(gated, p + 1)
                dve.tensor_copy(logits[:, p, :], slot[2][:, 0:E]).then_inc(logits_ready, 1)


            def step(b, u, half, stages):
                proj, sco, val, tail, end = stages
                n, p, t, e, w = b + 1, b - 1, b - 2, b - 3, 1 - u
                if end:
                    row_max2(e)
                if sco:
                    row_max(b, 0)
                if end:
                    invert_sum2(e)
                if sco:
                    row_max(b, 1)
                    row_max(b, 2)
                    row_max(b, 3)
                if end:
                    residual2(e, w)
                if sco:
                    keep_max_high(b)
                if end:
                    stats_of_t2(e)
                if sco:
                    keep_max_low(b)
                if tail:
                    residual1(t, u)
                if end:
                    moments_of_t2(e)
                if tail:
                    stats_of_t1(t)
                    moments_of_t1(t)
                if end:
                    norm2(e)
                if tail:
                    norm1(t, u)
                if end:
                    keep_logits(e)
                if val:
                    invert_sums(p)
                    normalise(p)

            batches(dve, step)

            def over_e(a):
                return a.unsqueeze(2).broadcast_to([P, B, E])

            dve.wait_ge(logits_ready, B)
            then(dve.tensor_reduce(ro_t[:, :], logits[:, :, :], AX.X, ALU.max))
            dve.tensor_tensor(tok_a[:, :, :], logits[:, :, :], over_e(ro_t[:, :]), ALU.subtract).then_inc(gate_max_ready, 1)
            dve.wait_ge(gate_exp, 1)
            then(dve.tensor_reduce(ro_t[:, :], tok_b[:, :, :], AX.X, ALU.add))
            then(dve.reciprocal(ro_u[:, :], ro_t[:, :]))
            then(dve.tensor_tensor(prob[:, :, :], tok_b[:, :, :], over_e(ro_u[:, :]), ALU.mult))
            dve.tensor_copy(ex_b[:, :].rearrange("p (b i e) -> p b i e", b=4, e=E),
                            prob[:, :, :].rearrange("p (i b) e -> p b i e", b=4)).then_inc(found, 1)

            then(dve.memset(keep[:, :], 0.0))
            for d in range(3):
                then(dve.memset(two_bits[:, d:d + 1], (d + 1) << (PROB_BITS - 2)))
            dve.wait_ge(gates_turned, 1)
            then(dve.tensor_copy(prob_e[:, :], score_bank[0][:, :]))
            base = steps[0]
            def search_step(i, d4, d1):
                dve.tensor_tensor(cand[:, :].bitcast(I32), thr.bitcast(I32).broadcast_to([P, 3]), two_bits[:, :],
                                  ALU.bitwise_or).then_inc(dve_step, 1)
                dve.wait_ge(dve_step, i * 12 + (d4 + 1))
                for d in range(3):
                    dve.tensor_scalar([ex_a, ex_b, ex_c][d][:, :], prob_e[:, :], cand[:, d:d + 1], None, ALU.is_ge,
                                      ALU.add, accum_out=cnt[:, d:d + 1]).then_inc(searched, 1)
                dve.tensor_scalar(two_bits[:, :], two_bits[:, :], 2, None, ALU.logical_shift_right).then_inc(dve_step, 1)
                dve.wait_ge(counted, i * 3 + (d1 + 1))
                dve.scalar_tensor_tensor(keep[:, 0:3], score_bank[1][:, 0:3], float(CAP), cand[:, :], ALU.is_ge,
                                         ALU.mult).then_inc(dve_step, 1)
                dve.wait_ge(dve_step, i * 12 + (d4 + 3))
                dve.tensor_reduce(thr, keep[:, :], AX.X, ALU.max).then_inc(dve_step, 1)
                dve.wait_ge(dve_step, i * 12 + (d4 + 4))

            with dve.Fori(0, PROB_BITS // 6) as i:
                for u in range(3):
                    search_step(i, base + 4 * u, u)
            steps[0] += 4 * (PROB_BITS // 2)

            dve.tensor_scalar(ex_a[:, :], prob_e[:, :], thr, None, ALU.is_gt, ALU.add,
                              accum_out=cnt[:, 0:1]).then_inc(searched, 1)
            dve.tensor_scalar(ex_b[:, :], prob_e[:, :], thr, None, ALU.is_equal, ALU.add,
                              accum_out=cnt[:, 1:2]).then_inc(searched, 1)
            dve.wait_ge(searched, PROB_BITS // 2 * 3 + 2)
            then(dve.tensor_tensor_scan(ex_c[:, :], cst[:, C_ONES:C_ONES + 1].broadcast_to([P, 512]),
                                        ex_b[:, :], 0.0, ALU.mult, ALU.add))
            dve.wait_ge(counted, PROB_BITS // 2 + 2)
            then(dve.tensor_scalar(need[:, :], score_bank[1][:, 0:1], -1.0, float(CAP), ALU.mult, ALU.add))
            then(dve.tensor_copy(before[:, :], score_bank[1][:, 1:2]))
            then(dve.tensor_scalar(ex_c[:, :], ex_c[:, :], before[:, 0:1], need[:, 0:1], ALU.add, ALU.is_le))
            then(dve.tensor_tensor(ex_c[:, :], ex_c[:, :], ex_b[:, :], ALU.mult))
            dve.tensor_tensor(ex_a[:, :], ex_a[:, :], ex_c[:, :], ALU.add).then_inc(found, 1)

            dve.wait_ge(sel_turned, 1)
            sel = tok_a
            sv = sel[:, :, :].rearrange("p (i b) e -> p b i e", b=4)
            kb = score_bank[0][:, :].rearrange("p (b i e) -> p b i e", b=4, e=E)
            then(dve.tensor_copy(sv, kb))
            then(dve.tensor_tensor(tok_b[:, :, :], prob[:, :, :], sel[:, :, :], ALU.mult))
            then(dve.scalar_tensor_tensor(tok_b[:, :, :], sel[:, :, :], -1.0, tok_b[:, :, :], ALU.add, ALU.add))
            then(dve.tensor_reduce(ro_t[:, :], tok_b[:, :, :], AX.X, ALU.max))
            then(dve.tensor_scalar(ro_u[:, :], ro_t[:, :], 0.0, None, ALU.is_lt))
            then(dve.tensor_tensor(tok_c[:, :, :], prob[:, :, :], over_e(ro_u[:, :]), ALU.mult))
            then(dve.tensor_scalar(ro_u[:, :], ro_u[:, :], -1.0, None, ALU.add))
            then(dve.tensor_tensor(tok_c[:, :, :], tok_c[:, :, :], over_e(ro_u[:, :]), ALU.add))
            then(dve.tensor_tensor(tok_b[:, :, :], tok_b[:, :, :], tok_c[:, :, :], ALU.max))
            then(dve.tensor_reduce(weight[:, :], tok_b[:, :, :], AX.X, ALU.max))
            then(dve.tensor_tensor(tok_b[:, :, :], tok_b[:, :, :], over_e(weight[:, :]), ALU.is_equal))
            desc = cst[:, C_DESC:C_DESC + E].unsqueeze(1).broadcast_to([P, B, E])
            then(dve.tensor_tensor(tok_b[:, :, :], tok_b[:, :, :], desc, ALU.mult))
            then(dve.tensor_reduce(ro_t[:, :], tok_b[:, :, :], AX.X, ALU.max))
            onehot = tok_c
            then(dve.tensor_tensor(onehot[:, :, :], tok_b[:, :, :], over_e(ro_t[:, :]), ALU.is_equal))
            dve.tensor_copy(onehot_bf[:, :, :], onehot[:, :, :].rearrange("p t e -> p e t")).then_inc(found, 1)

            dve.wait_ge(ranked, 1)
            ends, totals = ex_b, ex_a
            then(dve.tensor_copy(totals[:, :], score_bank[2][:, :]))
            then(dve.tensor_tensor_scan(ends[:, :], cst[:, C_ONES:C_ONES + 1].broadcast_to([P, 512]),
                                        totals[:, :], 0.0, ALU.mult, ALU.add))
            then(dve.tensor_tensor(totals[:, :], ends[:, :], totals[:, :], ALU.subtract))
            start_e = totals[:, :].rearrange("p (e t) -> p e t", e=E)[:, :, 0]
            end_e = ends[:, :].rearrange("p (e t) -> p e t", e=E)[:, :, B - 1]
            then(dve.tensor_tensor(e_f[0][:, :], end_e, start_e, ALU.subtract))
            then(dve.tensor_scalar(e_f[0][:, :], e_f[0][:, :], float(P - 1), None, ALU.add))
            then(dve.tensor_copy(e_i[:, :], e_f[0][:, :]))
            then(dve.tensor_scalar(e_i2[:, :], e_i[:, :], 7, None, ALU.logical_shift_right))
            then(dve.tensor_copy(e_f[1][:, :], e_i2[:, :]))
            then(dve.tensor_tensor_scan(e_f[2][:, :], cst[:, C_ONES:C_ONES + E], e_f[1][:, :], 0.0,
                                        ALU.mult, ALU.add))
            then(dve.tensor_tensor(e_f[3][:, :], e_f[2][:, :], e_f[1][:, :], ALU.subtract))
            then(dve.scalar_tensor_tensor(e_f[4][:, :], e_f[3][:, :], float(P), start_e, ALU.mult, ALU.subtract))
            then(dve.tensor_tensor(totals[:, :], score_bank[1][:, :], totals[:, :], ALU.add))
            slots = ex_c[:, :].rearrange("p (e t) -> p e t", e=E)
            then(dve.tensor_tensor(slots, totals[:, :].rearrange("p (e t) -> p e t", e=E),
                                   e_f[4][:, :].unsqueeze(2).broadcast_to([P, E, B]), ALU.add))
            then(dve.tensor_tensor(tok_a[:, :, :], slots.rearrange("p e t -> p t e"), onehot[:, :, :], ALU.mult))
            then(dve.tensor_reduce(pos_f[:, :], tok_a[:, :, :], AX.X, ALU.add))
            dve.wait_ge(row_kept, B)
            then(dve.tensor_copy(rows[:, :, D], weight[:, :]))
            then(dve.tensor_copy(rows[:, :, D + 1], cst[:, C_TOK:C_TOK + B]))

            def stage(t, r):
                dve.tensor_copy(row_stage[r][:, :], rows[:, t, :]).then_inc(staged[r], 1)
                dve.tensor_copy(pos_stage[r][:, :], pos_f[:, bass.ds(t, 1)]).then_inc(staged[r], 1)

            for t in range(RS):
                stage(t, t)
            with dve.Fori(1, B // RS) as i:
                for r in range(RS):
                    dve.wait_ge(scattered[r], i * 16)
                    stage(i * RS + r, r)

            then(dve.memset(tile_e[:, :], 0.0))
            then(dve.tensor_tensor(tile_cmp[:, :, :],
                                   cst[:, C_TILE:C_TILE + NT].unsqueeze(2).broadcast_to([P, NT, E - 1]),
                                   e_f[2][:, 0:E - 1].unsqueeze(1).broadcast_to([P, NT, E - 1]), ALU.is_ge))
            then(dve.tensor_reduce(tile_e[:, 1:1 + NT], tile_cmp[:, :, :], AX.X, ALU.add))
            then(dve.tensor_copy(tile_i[:, :], tile_e[:, :]))
            eights = tile_e[:, 0:8 * NW].rearrange("p (w k) -> p w k", k=8)
            then(dve.tensor_tensor(eights, eights, cst[:, C_DIGIT:C_DIGIT + 8].unsqueeze(1).broadcast_to([P, NW, 8]),
                                   ALU.mult))
            then(dve.tensor_reduce(low_digits[:, :], eights, AX.X, ALU.add))
            then(dve.tensor_copy(words[0][:, :], low_digits[:, :]))
            for d in range(2):
                digit = tile_i[:, 8:8 * NW + 8].rearrange("p (w k) -> p w k", k=8)[:, :, d]
                then(dve.tensor_scalar(words[1 + d][:, :], digit, 3 * (8 + d), None, ALU.logical_shift_left))
            then(dve.tensor_tensor(words[3][:, :], words[0][:, :], words[1][:, :], ALU.bitwise_or))
            dve.tensor_tensor(words[4][:, :], words[3][:, :], words[2][:, :], ALU.bitwise_or).then_inc(table_ready, 1)

            def add_rows(j, v, eight):
                ge(dve, y2_ready[v], eight)
                dve.wait_ge(y_made, j + 1)
                dve.scalar_tensor_tensor(y1[v][:, :], y_bank[v % 2][:, 0:D], xs[v][:, D:D + 1], xs[v][:, 0:D],
                                         ALU.mult, ALU.add).then_inc(y1_ready, 1)

            def keep_tokens(k, v, eight):
                ge(dve, out_stored[v], eight * 16)
                dve.tensor_copy(tok_i[v][:, :], xs[v][:, D + 1:D + 2]).then_inc(tok_ready, 1)

            def measure(j, v):
                dve.wait_ge(y1_ready, j + 1)
                dve.bn_stats(stats3[v % 2][:, :], y1[v][:, :]).then_inc(st3_ready, 1)

            def moments(j, v):
                alone(dve)
                dve.wait_ge(st3_ready, j + 1)
                dve.bn_aggr(mv3[:, v, :], stats3[v % 2][:, :]).then_inc(mv3_ready, 1)

            def normalise_rows(k, v, four, eight):
                dve.wait_ge(rstd3_ready, four + 1)
                ge(dve, out_stored[v], eight * 16)
                dve.tensor_scalar(y2[v][:, :], y1[v][:, :], mv3[:, v, 0:1], rstd3[:, v:v + 1], ALU.subtract,
                                  ALU.mult).then_inc(y2_ready[v], 1)

            def ffn(j, v, four, eight):
                add_rows(j, v, eight)
                if not (isinstance(j, int) and j < 1):
                    keep_tokens(j - 1, (v + 7) % 8, eight + (v - 1) // 8)
                measure(j, v)
                if not (isinstance(j, int) and j < 6):
                    normalise_rows(j - 6, (v + 2) % 8, four(-6), eight + (v - 6) // 8)
                moments(j, v)

            tiles(dve, ffn, 2)
            for k in range(NT - 1, NT):
                keep_tokens(k, k % 8, k // 8)
            for k in range(NT - 6, NT):
                normalise_rows(k, k % 8, k // 4, k // 8)

        @block.scalar
        def _(act):
            for dst, src in ((cst[:, :], consts), (wq_sb[:, :, :], wq), (wk_sb[:, :, :], wk), (wv_sb[:, :], wv),
                             (wo_sb[:, :], wo), (bq_sb[:, :], bq), (bk_sb[:, :], bk), (sl_sb[:, :], slopes),
                             (bv_sb[:, :], bv), (bo_sb[:, :], bo), (wg_sb[:, :], wg)):
                act.dma_start(dst, src).then_inc(weights_in, 16)
            for dst, src in ((w1_sb[:, 0:4, :], w1[0:4].rearrange("e d f -> d e f")),
                             (w1_sb[:, 4:8, :], w1[4:8].rearrange("e d f -> d e f")),
                             (w2_sb[:, :, 0, :], w2[:, 0:P, :].rearrange("e f d -> f e d")),
                             (w2_sb[:, :, 1, :], w2[:, P:F, :].rearrange("e f d -> f e d"))):
                act.dma_start(dst, src).then_inc(ffn_weights_in, 16)
            act.wait_ge(blank_made, 4)
            parts = sorted_rows[:, :].rearrange("(k n p) r -> k p n r", k=BLANK_PARTS, p=P)
            for k in range(BLANK_PARTS):
                act.dma_start(parts[k], blank_row[:, :].unsqueeze(1).broadcast_to(
                    [P, NT // BLANK_PARTS, ROW])).then_inc(blanks_out, 16)

            def keep_values(n, u):
                act.wait_ge(v_made, n + 1)
                nc.scalar.activation(v_sb[u][:, :, HD:2 * HD],
                                     value_bank[:, 2 * P:3 * P].rearrange("p (h d) -> p h d", h=H),
                                     ACT.Copy).then_inc(v_ready, 1)

            q_low_rows, k_low_rows = cst[:, C_LOW + 2:C_LOW + 3], cst[:, C_LOW + 3:C_LOW + 4]

            def tiled(bank_):
                return bank_[:, :].rearrange("p (c t) -> p c t", c=NC_)

            def round_keys(n):
                act.wait_ge(k_made, n + 1)
                nc.scalar.activation(k_high[:, :, :], tiled(proj_bank), ACT.Identity,
                                     scale=k_low_rows).then_inc(k_high_ready, 1)

            def round_queries(n):
                act.wait_ge(q_made, n + 1)
                nc.scalar.activation(q_high[:, :, :], tiled(query_bank), ACT.Identity,
                                     scale=q_low_rows).then_inc(q_high_ready, 1)

            def keep_keys(n, u):
                act.wait_ge(k_split, n + 1)
                nc.scalar.activation(kt[u][:, :, :], tiled(proj_bank), ACT.Copy).then_inc(k_ready, 1)

            def keep_queries(n, u):
                act.wait_ge(q_split, n + 1)
                nc.scalar.activation(qt[u][:, :, :], tiled(query_bank), ACT.Copy).then_inc(q_ready, 1)

            def keep_less_max(b):
                act.wait_ge(max_added, b + 1)
                nc.scalar.activation(q_less_max[:, :, :], query_bank[:, :].rearrange("p (c t) -> p c t", c=NC_),
                                     ACT.Copy).then_inc(qm_ready, 1)

            def keep_sums(p):
                act.wait_ge(summed, p + 1)
                nc.scalar.activation(sums[:, :, :], value_bank[:, 0:2 * P].rearrange("p (t q) -> p t q", t=2),
                                     ACT.Copy).then_inc(sums_ready, 1)

            def keep_x1t(p):
                act.wait_ge(x1_turned, p + 1)
                nc.scalar.activation(x1t[:, :], slot[1], ACT.Copy, scale=D ** -0.5).then_inc(x1t_ready, 1)

            def exp2(p):
                act.wait_ge(max2_ready, p + 1)
                nc.scalar.activation(p2[:, :], slot[0][:, 0:SK], ACT.Exp, bias=neg_max2[:, 0:1],
                                     accum_out=sum2[:, :]).then_inc(p2_ready, 1)

            def keep_p2t(p):
                act.wait_ge(p2_turned, p + 1)
                nc.scalar.activation(p2t[:, :], slot[1][0:SK, :], ACT.Copy).then_inc(p2t_ready, 1)

            def exp(b, g):
                act.wait_ge(rescored, 4 * b + ORDER.index(g) + 1)
                nc.scalar.activation(probs_t[:, g, :], score_bank[g][:, :], ACT.Exp).then_inc(probs_ready, 1)

            def keep_x2t(p):
                act.wait_ge(x2_turned, p + 1)
                nc.scalar.activation(x2t[:, :], slot[0], ACT.Copy).then_inc(x2t_ready, 1)

            act.wait_ge(prep, 2)
            keep_values(0, 0)
            round_keys(0)
            round_queries(0)
            keep_keys(0, 0)
            keep_queries(0, 0)

            def step(b, u, half, stages):
                proj, sco, val, tail, end = stages
                n, p, t, e, w = b + 1, b - 1, b - 2, b - 3, 1 - u
                if end:
                    exp2(e)
                    keep_p2t(e)
                if proj:
                    round_keys(n)
                if val:
                    keep_sums(p)
                if proj:
                    keep_values(n, w)
                if sco:
                    keep_less_max(b)
                if proj:
                    keep_keys(n, w)
                if end:
                    keep_x2t(e)
                if proj:
                    round_queries(n)
                if sco:
                    exp(b, ORDER[0])
                    exp(b, ORDER[1])
                if tail:
                    keep_x1t(t)
                if proj:
                    keep_queries(n, w)
                if sco:
                    exp(b, ORDER[2])
                    exp(b, ORDER[3])

            batches(act, step)

            act.wait_ge(gate_max_ready, 1)
            nc.scalar.activation(tok_b[:, :, :], tok_a[:, :, :], ACT.Exp).then_inc(gate_exp, 1)

            def keep_rows_t(j, u2):
                act.wait_ge(xs_turned, j + 1)
                ge(act, hid_made, j - 1)
                nc.scalar.activation(xs_t[u2][:, :], score_bank[u2][:, 0:P], ACT.Copy).then_inc(xs_t_ready, 1)

            def gelu(j, u2):
                act.wait_ge(hid_made, j + 1)
                ge(act, hid_turned, j - 1)
                nc.scalar.activation(hid[u2][:, :], score_bank[2 + u2][:, 0:F], ACT.Gelu).then_inc(hid_ready, 1)

            def keep_hidden_t(j, u2):
                act.wait_ge(hid_turned, j + 1)
                ge(act, y_made, j - 1)
                nc.scalar.activation(hid_t[u2][:, :, :], ht_bank[u2][:, 0:F].rearrange("p (c t) -> p c t", c=2),
                                     ACT.Copy).then_inc(hid_t_ready, 1)

            keep_rows_t(0, 0)
            keep_rows_t(1, 1)

            def ffn(j, v, four, eight):
                inside = not isinstance(j, int)
                if inside or j + 2 < NT:
                    keep_rows_t(j + 2, v % 2)
                if not inside and j == 0:
                    gelu(0, 0)
                if inside or j + 1 < NT:
                    gelu(j + 1, (v + 1) % 2)
                keep_hidden_t(j, v % 2)

            tiles(act, ffn, 1)

        @block.gpsimd
        def _(pool):
            pool.memset(blank_row[:, 0:ROW - 1], 0.0).then_inc(blank_made, 1)
            pool.memset(blank_row[:, ROW - 1:ROW], float(2 * T)).then_inc(blank_made, 1)
            pool.memset(neg_half[:, :], -0.5).then_inc(blank_made, 1)
            pool.memset(eps[:, :], EPS).then_inc(blank_made, 1)
            pool.wait_ge(blank_made, 4)

            def rstd(mv, ve, r, have, mid, done, n):
                pool.wait_ge(have, n)
                pool.tensor_tensor(ve[:, :], mv[:, 1:2], eps[:, 0:1], ALU.add).then_inc(mid, 1)
                pool.wait_ge(mid, n)
                pool.tensor_tensor(r[:, :], ve[:, :], neg_half[:, 0:1], ALU.pow).then_inc(done, 1)

            def add_bias(b, u, loads):
                pool.wait_ge(back_in[u], loads * 16)
                pool.tensor_tensor(x_plus_bias[u][:, :], x_sb[u][:, :], out_bias[:, :], ALU.add).then_inc(xb_ready, 1)

            def keep_row(p):
                alone(pool)
                pool.wait_ge(x2_ready, p + 1)
                pool.tensor_copy(rows[:, p, 0:D], x2[:, :]).then_inc(row_kept, 1)

            pool.wait_ge(weights_in, N_WEIGHTS)
            pool.wait_ge(prep, 3)

            def step(b, u, half, stages):
                proj, sco, val, tail, end = stages
                p, t, e = b - 1, b - 2, b - 3
                if val:
                    add_bias(p, 1 - u, half(-1) + 1)
                if end:
                    rstd(mv2, ve2, rstd2, mv2_ready, ve2_ready, rstd2_ready, e + 1)
                if tail:
                    rstd(mv1, ve1, rstd1, mv1_ready, ve1_ready, rstd1_ready, t + 1)
                if end:
                    keep_row(e)

            batches(pool, step)

            pool.wait_ge(blanks_out, 16 * BLANK_PARTS)
            last_slot = pool.to_reg(NT * P - 1)
            with pool.Fori(2, 2 * (B // RS) + 2, 2) as both:
                for r in range(RS):
                    alone(pool)
                    pool.wait_ge(staged[r], both)
                    pool.indirect_dma_start(out=sorted_rows[:, :],
                                            out_offset=bass.IndirectOffsetOnAxis(ap=pos_stage[r][:, 0:1], axis=0),
                                            in_=row_stage[r][:, :], in_offset=None, bounds_check=last_slot,
                                            oob_is_err=False).then_inc(scattered[r], 16)

            last_token = pool.to_reg(T - 1)

            def rstd_of_four(g, h):
                four = slice(4 * h, 4 * h + 4)
                pool.wait_ge(mv3_ready, g * 4 + 4)
                pool.tensor_tensor(ve3[:, four], mv3[:, four, 1], eps[:, :], ALU.add).then_inc(ve3_ready, 1)
                pool.wait_ge(ve3_ready, g + 1)
                pool.tensor_tensor(rstd3[:, four], ve3[:, four], neg_half[:, :], ALU.pow).then_inc(rstd3_ready, 1)

            def store_eight(n):
                last = isinstance(n, int) and n == NT // 8
                for v in range(8):
                    alone(pool)
                    pool.wait_ge(y2_ready[v], n)
                    pool.indirect_dma_start(out=out, out_offset=bass.IndirectOffsetOnAxis(ap=tok_i[v][:, 0:1], axis=0),
                                            in_=y2[v][:, :], in_offset=None, bounds_check=last_token,
                                            oob_is_err=False).then_inc(out_stored[v], 16)
                    if v == 1:
                        rstd_of_four(n * 2 - 1, 1)
                    if v == 5 and not last:
                        rstd_of_four(n * 2, 0)

            rstd_of_four(0, 0)
            with pool.Fori(1, NT // 8) as n:
                store_eight(n)
            store_eight(NT // 8)
            for v in range(8):
                pool.wait_ge(out_stored[v], 16 * (NT // 8))


def constants():
    c = np.zeros((P, C_N), np.float32)
    p = np.arange(P)
    row = p % 32
    c[:, C_ID:C_ID + P] = np.eye(P)
    c[:, C_TQ:C_TQ + P] = np.where(((row == POS_ROW) | (row == POS_ROW + 1))[:, None], -p[None, :], 1)
    c[:, C_KAUG:C_KAUG + P] = np.where(((row == SLOPE_ROW) | (row == SLOPE_ROW + 1))[:, None], p[None, :],
                                       ((row >= POS_ROW) & (row < MAX_ROW + 2))[:, None])
    c[:, C_ROWS:C_ROWS + P] = np.diag(row < BIAS_ROW)
    for t in range(NC_):
        c[:, C_BIAS + P * t:C_BIAS + P * (t + 1)] = ((row >= BIAS_ROW) & (p // 32 == t))[:, None]
    c[:, C_LOW] = (row == SLOPE_ROW + 1) | (row == POS_ROW + 1)
    c[:, C_LOW + 1] = row == BIAS_ROW + 1
    c[:, C_LOW + 2] = row // HD == 2
    c[:, C_LOW + 3] = row // HD == 1
    g = p // 32
    for base, up in ((C_V, 0), (C_D, 2 * HD)):
        for t in range(2):
            mine = row // (2 * HD) == t
            c[(32 * g + up + row % (2 * HD))[mine], base + P * t + p[mine]] = 1
    same = p[:, None] % E == p[None, :] % E
    c[:, C_SAME:C_SAME + P] = same
    c[:, C_BELOW:C_BELOW + P] = same & (p[:, None] < p[None, :])
    c[:, C_TRI:C_TRI + P] = p[:, None] < p[None, :]
    c[:, C_DESC:C_DESC + E] = E - np.arange(E)
    c[:, C_TILE:C_TILE + NT] = np.arange(NT)
    c[:, C_ONES:C_ONES + P] = 1
    c[:, C_TOK:C_TOK + T // P] = p[:, None] + P * np.arange(T // P)[None, :]
    c[:, C_DIGIT:] = 8 ** np.arange(8)
    return c


def kernel(**inputs):
    import concourse.bacc as bacc
    from concourse.bass_utils import run_bass_kernel_spmd

    a = {k: np.asarray(v) for k, v in inputs.items()}
    x, ctx = a["x"], a["ctx_1024"]
    slopes = np.zeros((NG, 32, NC_), np.float32)
    slopes[:, SLOPE_ROW:POS_ROW + 2] = a["L0_attn_slopes"].reshape(NG, 1, NC_)
    def by_heads(m):
        tiled = np.zeros((m.shape[0], NC_, NG, 4, HD), np.float32)
        tiled[:, :, :, :3] = m.reshape(m.shape[0], NG, NC_, 1, HD).transpose(0, 2, 1, 3, 4)
        return tiled.reshape(m.shape[0], NC_, P)

    def bias_rows(b):
        rows_ = np.zeros((NG, 32, P), np.float32)
        rows_[:, BIAS_ROW:] = by_heads(b.reshape(1, P))[0][:, None]
        return rows_.reshape(P, P)

    arrays = {
        "x": x, "xt": x.transpose(0, 2, 1), "ctx": ctx, "ctxt": ctx.transpose(0, 2, 1),
        "wq": by_heads(a["L0_attn_Wq"].T), "wk": by_heads(a["L0_attn_Wk"].T), "wv": a["L0_attn_Wv"].T, "wo": a["L0_attn_Wo"].T,
        "bq": bias_rows(a["L0_attn_bq"]), "bk": bias_rows(a["L0_attn_bk"]), "slopes": slopes.reshape(P, NC_),
        "bv": a["L0_attn_bv"].reshape(P, 1), "bo": a["L0_attn_bo"].reshape(1, P),
        "wg": a["L0_ffn_Wg"], "w1": a["L0_ffn_W1"], "w2": a["L0_ffn_W2"], "consts": constants(),
    }
    nc = bacc.Bacc("TRN2", target_bir_lowering=False, num_devices=1)
    arrays = {f"in_{k}": np.ascontiguousarray(v) for k, v in arrays.items()}
    args = [nc.dram_tensor(k, v.shape, mybir.dt.from_np(v.dtype), kind="ExternalInput").ap() for k, v in arrays.items()]
    result = nc.dram_tensor("result", (T, D), F32, kind="ExternalOutput").ap()
    attention_ffn(nc, *args, result)
    r = run_bass_kernel_spmd(nc, [arrays], core_ids=[0])
    return r.results[0]["result"].reshape(B, S, D)
```
